# Optimizing a Trainium2 kernel written in Bass

```python
import numpy as np
import jax
import jax.numpy as jnp

def _softmax(x, axis=-1):
    return jax.nn.softmax(x, axis=axis)

def _gelu(x):
    return jax.nn.gelu(x, approximate=True)

def _silu(x):
    return jax.nn.silu(x)

def _sigmoid(x):
    return jax.nn.sigmoid(x)

def _layernorm(x, axis=-1, eps=1e-05):
    m = jnp.mean(x, axis=axis, keepdims=True)
    v = jnp.var(x, axis=axis, keepdims=True)
    return (x - m) / jnp.sqrt(v + eps)

def _scatter_add(tgt, idx, src, axis=0):
    return tgt.at[idx].add(src)

def _segment_sum(src, seg, n):
    return jax.ops.segment_sum(src, seg, n)
kernel_name = 'mk_lm_tower_d1_tok_ids768_r4_014882'

def setup_inputs(seed: int=0):
    np.random.seed(seed)
    _w = jnp.asarray

    def _rec_inputs():
        import jax
        import jax.numpy as jnp
        _rk = jax.random.key(seed)
        x = jax.random.randint(jax.random.fold_in(_rk, 1), (64, 128), 0, 31993, jnp.int32)
        return x
    x = _rec_inputs()

    def _L0_tok_setup():
        import jax, jax.numpy as jnp
        import numpy as np
        NUM_HEADS = 12
        EPS = 1e-05

        def _layer_norm(x, gamma, beta):
            mean = jnp.mean(x, axis=-1, keepdims=True)
            std = jnp.sqrt(jnp.mean((x - mean) ** 2, axis=-1, keepdims=True))
            return (x - mean) / (std + EPS) * gamma + beta

        def _pos_encoding(L, D, dtype):
            pos = jnp.arange(L, dtype=dtype)[:, None]
            i = jnp.arange(D, dtype=dtype)[None, :]
            ang = pos / jnp.power(jnp.asarray(10000.0, dtype), 2.0 * i / D)
            even = jnp.arange(D) % 2 == 0
            return jnp.where(even[None, :], jnp.cos(ang), jnp.sin(ang))
        key = jax.random.key(seed)
        ks = jax.random.split(key, 12)
        B, L, D, F, V = (4, 512, 192, 768, 8000)
        s = lambda d: 1.0 / np.sqrt(d)
        return {'tokens': jax.random.randint(ks[0], (B, L), 0, V, dtype=jnp.int32), 'emb': jax.random.normal(ks[1], (V, D), jnp.float32) * 0.02, 'wq': jax.random.normal(ks[2], (D, D), jnp.float32) * s(D), 'bq': jnp.zeros((D,), jnp.float32), 'wk': jax.random.normal(ks[3], (D, D), jnp.float32) * s(D), 'bk': jnp.zeros((D,), jnp.float32), 'wv': jax.random.normal(ks[4], (D, D), jnp.float32) * s(D), 'bv': jnp.zeros((D,), jnp.float32), 'wo': jax.random.normal(ks[5], (D, D), jnp.float32) * s(D), 'bo': jnp.zeros((D,), jnp.float32), 'w1': jax.random.normal(ks[6], (D, F), jnp.float32) * s(D), 'b1': jnp.zeros((F,), jnp.float32), 'w2': jax.random.normal(ks[7], (F, D), jnp.float32) * s(F), 'b2': jnp.zeros((D,), jnp.float32), 'gamma1': jnp.ones((D,), jnp.float32), 'beta1': jnp.zeros((D,), jnp.float32), 'gamma2': jnp.ones((D,), jnp.float32), 'beta2': jnp.zeros((D,), jnp.float32)}
    _L0_tok_all = _L0_tok_setup()
    _L0_tok_in = {k: v for k, v in _L0_tok_all.items() if k in ('emb', 'wq', 'bq', 'wk', 'bk', 'wv', 'bv', 'wo', 'bo', 'w1', 'b1', 'w2', 'b2', 'gamma1', 'beta1', 'gamma2', 'beta2')}
    del _L0_tok_all

    def _L0_attn_setup():
        import jax, jax.numpy as jnp
        import numpy as np
        B, N, DIM = (8, 256, 192)
        H = 12
        HD = DIM // H
        key = jax.random.key(seed)
        k1, k2, k3 = jax.random.split(key, 3)
        x = jax.random.normal(k1, (B, N, DIM), dtype=jnp.float32)
        scale = 1.0 / np.sqrt(DIM)
        Wq = jax.random.uniform(k2, (H * HD, DIM), dtype=jnp.float32, minval=-scale, maxval=scale)
        Wk = jax.random.uniform(k3, (H * HD, DIM), dtype=jnp.float32, minval=-scale, maxval=scale)
        betas = jnp.full((H,), HD ** (-0.5), dtype=jnp.float32)
        return {'x': x, 'Wq': Wq, 'Wk': Wk, 'betas': betas}
    _L0_attn_all = _L0_attn_setup()
    _L0_attn_in = {k: v for k, v in _L0_attn_all.items() if k in ('Wq', 'Wk', 'betas')}
    del _L0_attn_all

    def _L0_ffn_setup():
        import jax, jax.numpy as jnp
        import numpy as np
        DECAY = 0.9
        EPS = 0.01
        TOP_K = 2
        key = jax.random.key(seed)
        k1, k2, k3, k4 = jax.random.split(key, 4)
        B, S, H, I, E = (4, 512, 192, 512, 8)
        return {'hidden_states': jax.random.normal(k1, (B, S, H), jnp.float32), 'router_w': jax.random.normal(k2, (E, H), jnp.float32) * 0.02, 'w1': jax.random.normal(k3, (E, I, H), jnp.float32) * 0.02, 'w2': jax.random.normal(k4, (E, H, I), jnp.float32) * 0.02}
    _L0_ffn_all = _L0_ffn_setup()
    _L0_ffn_in = {k: v for k, v in _L0_ffn_all.items() if k in ('router_w', 'w1', 'w2')}
    del _L0_ffn_all
    return {'x': x, 'L0_tok_emb': _L0_tok_in['emb'], 'L0_tok_wq': _L0_tok_in['wq'], 'L0_tok_bq': _L0_tok_in['bq'], 'L0_tok_wk': _L0_tok_in['wk'], 'L0_tok_bk': _L0_tok_in['bk'], 'L0_tok_wv': _L0_tok_in['wv'], 'L0_tok_bv': _L0_tok_in['bv'], 'L0_tok_wo': _L0_tok_in['wo'], 'L0_tok_bo': _L0_tok_in['bo'], 'L0_tok_w1': _L0_tok_in['w1'], 'L0_tok_b1': _L0_tok_in['b1'], 'L0_tok_w2': _L0_tok_in['w2'], 'L0_tok_b2': _L0_tok_in['b2'], 'L0_tok_gamma1': _L0_tok_in['gamma1'], 'L0_tok_beta1': _L0_tok_in['beta1'], 'L0_tok_gamma2': _L0_tok_in['gamma2'], 'L0_tok_beta2': _L0_tok_in['beta2'], 'L0_attn_Wq': _L0_attn_in['Wq'], 'L0_attn_Wk': _L0_attn_in['Wk'], 'L0_attn_betas': _L0_attn_in['betas'], 'L0_ffn_router_w': _L0_ffn_in['router_w'], 'L0_ffn_w1': _L0_ffn_in['w1'], 'L0_ffn_w2': _L0_ffn_in['w2']}

def reference(x, L0_tok_emb, L0_tok_wq, L0_tok_bq, L0_tok_wk, L0_tok_bk, L0_tok_wv, L0_tok_bv, L0_tok_wo, L0_tok_bo, L0_tok_w1, L0_tok_b1, L0_tok_w2, L0_tok_b2, L0_tok_gamma1, L0_tok_beta1, L0_tok_gamma2, L0_tok_beta2, L0_attn_Wq, L0_attn_Wk, L0_attn_betas, L0_ffn_router_w, L0_ffn_w1, L0_ffn_w2):
    import jax
    import jax.numpy as jnp

    def _L0_tok_ref(tokens, emb, wq, bq, wk, bk, wv, bv, wo, bo, w1, b1, w2, b2, gamma1, beta1, gamma2, beta2):
        import jax, jax.numpy as jnp
        import numpy as np
        NUM_HEADS = 12
        EPS = 1e-05

        def _layer_norm(x, gamma, beta):
            mean = jnp.mean(x, axis=-1, keepdims=True)
            std = jnp.sqrt(jnp.mean((x - mean) ** 2, axis=-1, keepdims=True))
            return (x - mean) / (std + EPS) * gamma + beta

        def _pos_encoding(L, D, dtype):
            pos = jnp.arange(L, dtype=dtype)[:, None]
            i = jnp.arange(D, dtype=dtype)[None, :]
            ang = pos / jnp.power(jnp.asarray(10000.0, dtype), 2.0 * i / D)
            even = jnp.arange(D) % 2 == 0
            return jnp.where(even[None, :], jnp.cos(ang), jnp.sin(ang))
        B, L = tokens.shape
        D = emb.shape[1]
        H = NUM_HEADS
        dh = D // H
        x = emb[tokens] + _pos_encoding(L, D, emb.dtype)

        def heads(t):
            return t.reshape(B, L, H, dh).transpose(0, 2, 1, 3)
        q = heads(x @ wq + bq)
        k = heads(x @ wk + bk)
        v = heads(x @ wv + bv)
        scores = jnp.einsum('bhqd,bhkd->bhqk', q, k) / jnp.sqrt(jnp.asarray(dh, x.dtype))
        weights = jax.nn.softmax(scores, axis=-1)
        attn = jnp.einsum('bhqk,bhkd->bhqd', weights, v)
        attn = attn.transpose(0, 2, 1, 3).reshape(B, L, D)
        attn_out = attn @ wo + bo
        h1 = _layer_norm(x + attn_out, gamma1, beta1)
        ff = jax.nn.relu(h1 @ w1 + b1) @ w2 + b2
        return _layer_norm(h1 + ff, gamma2, beta2)

    def _L0_attn_ref(x, Wq, Wk, betas):
        import jax, jax.numpy as jnp
        import numpy as np
        B, N, DIM = (8, 256, 192)
        H = 12
        HD = DIM // H
        Q = jnp.einsum('bnd,hzd->bhnz', x, Wq.reshape(H, HD, DIM))
        K = jnp.einsum('bnd,hzd->bhnz', x, Wk.reshape(H, HD, DIM))
        Wqr = Wq.reshape(H, HD, DIM)
        Wkr = Wk.reshape(H, HD, DIM)
        F1 = jnp.einsum('hzd,bhkz->bkhd', Wqr, K)
        F2 = jnp.einsum('hzd,bhqz->bqhd', Wkr, Q)
        scores = jnp.einsum('bhqz,bhkz->bhqk', Q, K) * betas[None, :, None, None]
        attn = jax.nn.softmax(scores, axis=-1)
        T1 = jnp.einsum('bkhd,bhqk->bqd', F1, attn)
        T2 = jnp.einsum('bqhd,bhqk->bkd', F2, attn)
        return T1 + T2

    def _L0_ffn_ref(hidden_states, router_w, w1, w2):
        import jax, jax.numpy as jnp
        import numpy as np
        DECAY = 0.9
        EPS = 0.01
        TOP_K = 2
        B, S, H = hidden_states.shape
        E = router_w.shape[0]
        flat = hidden_states.reshape(B * S, H)
        logits = flat @ router_w.T
        probs = jax.nn.softmax(logits, axis=-1)
        topk_probs, topk_idx = jax.lax.top_k(probs, TOP_K)
        importance = jax.lax.stop_gradient(probs).sum(axis=0)
        running = jnp.ones((E,), dtype=flat.dtype)
        blended = running + (1.0 - DECAY) * (importance - running)
        running = blended + EPS
        balance = running[topk_idx]
        balanced = topk_probs / balance
        balanced = balanced / balanced.sum(axis=-1, keepdims=True)
        h = jnp.einsum('th,eih->tei', flat, w1)
        h = jax.nn.silu(h)
        outs = jnp.einsum('tei,ehi->teh', h, w2)
        sel = jnp.take_along_axis(outs, topk_idx[:, :, None], axis=1)
        combined = (sel * balanced[..., None]).sum(axis=1)
        return combined.reshape(B, S, H)
    h = _L0_tok_ref(x, L0_tok_emb, L0_tok_wq, L0_tok_bq, L0_tok_wk, L0_tok_bk, L0_tok_wv, L0_tok_bv, L0_tok_wo, L0_tok_bo, L0_tok_w1, L0_tok_b1, L0_tok_w2, L0_tok_b2, L0_tok_gamma1, L0_tok_beta1, L0_tok_gamma2, L0_tok_beta2)
    h = h + _L0_attn_ref(_layernorm(h, axis=-1), L0_attn_Wq, L0_attn_Wk, L0_attn_betas)
    h = h + _L0_ffn_ref(_layernorm(h, axis=-1), L0_ffn_router_w, L0_ffn_w1, L0_ffn_w2)
    return h

_drawn_inputs = setup_inputs


def setup_inputs(seed=0):
    import zlib

    import numpy as np

    out = dict(_drawn_inputs(seed))
    spreads = {'L0_tok_bq': (0.0, 2.0),
     'L0_tok_bk': (0.0, 2.0),
     'L0_tok_bv': (0.0, 0.1),
     'L0_tok_bo': (0.0, 0.1),
     'L0_tok_b1': (0.0, 0.1),
     'L0_tok_b2': (0.0, 0.1),
     'L0_tok_gamma1': (1.0, 0.2),
     'L0_tok_beta1': (0.0, 0.1),
     'L0_tok_gamma2': (1.0, 0.2),
     'L0_tok_beta2': (0.0, 0.1),
     'L0_attn_betas': (0.25, 0.6)}
    factors = {}
    for name, (base, spread) in spreads.items():
        noise = np.random.default_rng([zlib.crc32(name.encode()), seed]).standard_normal(out[name].shape)
        drawn = base * np.exp(spread * noise) if base else spread * noise
        out[name] = jnp.asarray(drawn.astype(out[name].dtype))
    for name, factor in factors.items():
        out[name] = (out[name] * factor).astype(out[name].dtype)
    return out
```

```python
from contextlib import ExitStack

import concourse.bass as bass
from concourse import mybir

ALU = mybir.AluOpType
ACT = mybir.ActivationFunctionType
AX = mybir.AxisListType
F32 = mybir.dt.float32
I32 = mybir.dt.int32
U32 = mybir.dt.uint32

P = 128
T = 64
D = 192
C = 96
NC = D // C
H = 12
HD = D // H
HC = C // HD
G = 32
HG = P // G
NG = H // HG
FF = 768
FM = FF // P
V = 8000
E = 8
EI = 512
EM = EI // P
EPS_TOK = 1e-05
EPS_LN = 1e-05
ROWS = ("bv", "bo", "b2", "gamma1", "beta1", "gamma2", "beta2")
SKEW = 3


def tower_kernel(nc, tok, emb, pe, ident, hmask, w_qkv, bqk, rows, wo, w1, b1, w2, wa, betas, wqk,
                 rw, m1, m2, out, scratch):
    ctx = ExitStack()
    with ctx:
        def sb(name, shape, dt=F32):
            return ctx.enter_context(nc.sbuf_tensor(name, shape, dt))

        def sem(name):
            return ctx.enter_context(nc.semaphore(name))

        tok_sb = sb("tok_sb", [P, T], I32)
        neg_sb = sb("neg_sb", [P, T], I32)
        pe_sb = sb("pe_sb", [P, D])
        id_sb = sb("id_sb", [P, P])
        mask_sb = sb("mask_sb", [C, HC])
        maska_sb = sb("maska_sb", [C, HC])
        maskb_sb = sb("maskb_sb", [C, NC, HC])
        betas_sb = sb("betas_sb", [C, NC])
        wqkv_sb = sb("wqkv_sb", [C, 3, NC, D])
        bqk_sb = sb("bqk_sb", [C, 2 * NC])
        rows_sb = sb("rows_sb", [P, len(ROWS), D])
        wo_sb = sb("wo_sb", [P, NG, D])
        w1_sb = sb("w1_sb", [C, NC, FF])
        b1_sb = sb("b1_sb", [P, FM])
        w2_sb = sb("w2_sb", [P, FM, D])
        wa_sb = sb("wa_sb", [C, 2, NC, D])
        wqk_sb = sb("wqk_sb", [P, NG, D])
        rw_sb = sb("rw_sb", [C, NC, E])
        m1_sb = sb("m1_sb", [C, NC, E * EI])
        m2_sb = sb("m2_sb", [P, EM, E, D])
        half_sb = sb("half_sb", [P, 1])
        tick_sb = sb("tick_sb", [P, 16])
        ptick_sb = sb("ptick_sb", [P, 1])
        ones_sb = sb("ones_sb", [P, P])
        iota_sb = sb("iota_sb", [P, E], U32)
        iotaf_sb = sb("iotaf_sb", [P, E])
        row = {name: rows_sb[:, i, :] for i, name in enumerate(ROWS)}

        h_all = sb("h_all", [P, T, D])
        probs_all = sb("probs_all", [P, T, E])
        idx_all = sb("idx_all", [P, T, 2], U32)

        idx_now = sb("idx_now", [P, 1], U32)
        xg = sb("xg", [P, D])
        x = sb("x", [P, D])
        xT = sb("xT", [C, NC * P])
        qkT = sb("qkT", [C, 2 * NC, P])
        kbd = sb("kbd", [C, NC, HC, P])
        vpad = sb("vpad", [P, H, G])
        prob = sb("prob", [P, H, P])
        probT = sb("probT", [P, H, P])
        nmax = sb("nmax", [P, H])
        lsum = sb("lsum", [P, H])
        rsum = sb("rsum", [P, H])
        oT = sb("oT", [P, NG * P])
        y = sb("y", [P, D])
        h1 = sb("h1", [P, D])
        h1T = sb("h1T", [C, NC * P])
        hid = sb("hid", [P, FM, P])
        z = sb("z", [P, D])
        hs = sb("hs", [P, D])
        h2 = sb("h2", [P, D])
        xn = sb("xn", [P, D])
        xnT = sb("xnT", [C, NC * P])
        qk2T = sb("qk2T", [C, 2 * NC, P])
        kbd2 = sb("kbd2", [C, NC, HC, P])
        kpad = sb("kpad", [P, H, G])
        qpad = sb("qpad", [P, H, G])
        prob2 = sb("prob2", [P, H, P])
        prob2T = sb("prob2T", [P, H, P])
        nmax2 = sb("nmax2", [P, H])
        lsum2 = sb("lsum2", [P, H])
        rsum2 = sb("rsum2", [P, H])
        aT = sb("aT", [P, NG * P])
        x2n = sb("x2n", [P, D])
        x2nT = sb("x2nT", [C, NC * P])
        lg = sb("lg", [P, 8])
        lgmax = sb("lgmax", [P, 1])
        lgsum = sb("lgsum", [P, 1])
        lginv = sb("lginv", [P, 1])
        pr = sb("pr", [P, E])
        top8 = sb("top8", [P, 8])
        idx8 = sb("idx8", [P, 8], U32)
        st = [sb(f"st{i}", [P, 6]) for i in range(4)]
        mv = [sb(f"mv{i}", [P, 2]) for i in range(4)]
        sd = [sb(f"sd{i}", [P, 1]) for i in range(4)]
        rstd = [sb(f"rstd{i}", [P, 1]) for i in range(4)]

        idxf = sb("idxf", [P, T, 2])
        imp = sb("imp", [P, E])
        rinv = sb("rinv", [P, E])
        one1 = probT[:, 0:4, :].rearrange("p h n -> p (h n)").rearrange("p (t e) -> p t e", e=E)
        one2 = probT[:, 4:8, :].rearrange("p h n -> p (h n)").rearrange("p (t e) -> p t e", e=E)
        csum = sb("csum", [P, T])
        comb = sb("comb", [P, T, E])
        xe = kbd[:, 0, 0:4, :].rearrange("p (s c) n -> p s (c n)", s=2)
        ehid = prob[:, 0:8, :].rearrange("p (s m) n -> p s (m n)", s=2)

        ps = ctx.enter_context(nc.psum_tensor("ps", [P, 8, 512], F32))
        flat = ps[:, :, :].rearrange("p b n -> p (b n)")
        SA = flat[:, 0:1536]
        SB = flat[:, 1536:3072]
        N0 = flat[:, 3072:3584]
        N1 = flat[:, 3584:4096]
        QK_A = SA[0:C, 0:512]
        V_A = SA[:, 512:704]
        XT_A = SA[0:C, 1024:1280]
        O_A = N0[:, 0:384]
        Y_A = N1[:, 0:192]
        H1T_A = N1[0:C, 192:448]
        Z_A = N0[:, 0:192]
        XNT_B = SB[0:C, 1280:1536]
        QK_B = SB[0:C, 0:512]
        TOK_B = SB[:, 512:896]
        A_B = SB[:, 512:896]
        U_B = SB[:, 1024:1216]
        X2T_B = SB[0:C, 0:256]
        LG_B = SB[:, 1024:1032]

        tok_in = sem("tok_in")
        consts_in = sem("consts_in")
        moe_in = sem("moe_in")
        setup = sem("setup")
        tok_step = sem("tok_step")
        tok_fixed = sem("tok_fixed")
        mask_step = sem("mask_step")
        idx_ready = sem("idx_ready")
        rows_in = sem("rows_in")
        x_ready = sem("x_ready")
        res_ready = sem("res_ready")
        xT_ps = sem("xT_ps")
        xT_ready = sem("xT_ready")
        qk_ps = sem("qk_ps")
        v_ps = sem("v_ps")
        qk_ready = sem("qk_ready")
        v_ready = sem("v_ready")
        kbd_ready = sem("kbd_ready")
        s_ps = sem("s_ps")
        nm_ready = sem("nm_ready")
        p_ready = sem("p_ready")
        r_ready = sem("r_ready")
        pn_ready = sem("pn_ready")
        pT_ps = sem("pT_ps")
        pT_lo = sem("pT_lo")
        pT_hi = sem("pT_hi")
        o_ps = sem("o_ps")
        o_ready = sem("o_ready")
        y_ps = sem("y_ps")
        y_read = sem("y_read")
        h1_ready = sem("h1_ready")
        h1T_ps = sem("h1T_ps")
        h1T_ready = sem("h1T_ready")
        fa_ps = sem("fa_ps")
        fb_ps = sem("fb_ps")
        hid_a = sem("hid_a")
        hid_b = sem("hid_b")
        z_ps = sem("z_ps")
        z_read = sem("z_read")
        z_ready = sem("z_ready")
        hs_ready = sem("hs_ready")
        h_ready = sem("h_ready")
        xn_ready = sem("xn_ready")
        xnT_ps = sem("xnT_ps")
        xnT_ready = sem("xnT_ready")
        qk2_ps = sem("qk2_ps")
        qk2_ready = sem("qk2_ready")
        kbd2_ready = sem("kbd2_ready")
        tok_ps = sem("tok_ps")
        tok_ready = sem("tok_ready")
        s2_ps = sem("s2_ps")
        nm2_ready = sem("nm2_ready")
        p2_ready = sem("p2_ready")
        r2_ready = sem("r2_ready")
        pn2_ready = sem("pn2_ready")
        p2T_ps = sem("p2T_ps")
        p2T_lo = sem("p2T_lo")
        p2T_hi = sem("p2T_hi")
        a_ps = sem("a_ps")
        aT_ready = sem("aT_ready")
        u_ps = sem("u_ps")
        u_read = sem("u_read")
        x2n_ready = sem("x2n_ready")
        x2nT_ps = sem("x2nT_ps")
        x2nT_ready = sem("x2nT_ready")
        stored = sem("stored")
        lg_ps = sem("lg_ps")
        lgmax_ready = sem("lgmax_ready")
        lgexp_ready = sem("lgexp_ready")
        lginv_ready = sem("lginv_ready")
        pr_ready = sem("pr_ready")
        top8_ready = sem("top8_ready")
        idx8_ready = sem("idx8_ready")
        probs_ready = sem("probs_ready")
        imp_ready = sem("imp_ready")
        imp_ps = sem("imp_ps")
        comb_step = sem("comb_step")
        comb_ready = sem("comb_ready")
        w1_done = sem("w1_done")
        eh_ready = sem("eh_ready")
        w2_done = sem("w2_done")
        acc_step = sem("acc_step")
        out_done = sem("out_done")
        xe_in = [sem(f"xe_in{j}") for j in range(2)]
        st_ready = [sem(f"st_ready{n}") for n in range(4)]
        mv_ready = [sem(f"mv_ready{n}") for n in range(4)]
        var_ready = [sem(f"var_ready{n}") for n in range(4)]
        std_ready = [sem(f"std_ready{n}") for n in range(4)]
        sd_ready = [sem(f"sd_ready{n}") for n in range(4)]
        rstd_ready = [sem(f"rstd_ready{n}") for n in range(4)]
        centred = [sem(f"centred{n}") for n in range(4)]
        scaled = [sem(f"scaled{n}") for n in range(4)]

        def later(n):
            return not isinstance(n, int) or n > 0

        def tiles(eng, body):
            for i in range(SKEW + 1):
                body(i)
            with eng.Fori(SKEW + 1, T) as i:
                body(i)
            for i in range(T, T + SKEW):
                body(i)

        def pairs(eng, body):
            body(0)
            with eng.Fori(1, T // 2) as i:
                body(i)

        def at(i, skew, stage):
            t = i - skew
            if isinstance(i, int) and not 0 <= t < T:
                return
            stage(t)

        block = ctx.enter_context(nc.Block())

        CONSTS = [(pe_sb[:], pe), (id_sb[:], ident), (mask_sb[:], hmask), (wqkv_sb[:], w_qkv),
                  (bqk_sb[:], bqk), (rows_sb[:], rows), (wo_sb[:], wo), (w1_sb[:], w1), (b1_sb[:], b1),
                  (w2_sb[:], w2), (wa_sb[:], wa), (betas_sb[:], betas), (wqk_sb[:], wqk), (rw_sb[:], rw)]

        @block.sync
        def _(sp):
            sp.dma_start(tok_sb[:], tok).then_inc(tok_in, 16)
            for dst, src in CONSTS:
                sp.dma_start(dst, src).then_inc(consts_in, 16)
            sp.dma_start(m1_sb[:], m1).then_inc(moe_in, 16)
            sp.dma_start(m2_sb[:], m2).then_inc(moe_in, 16)

            def store(t):
                sp.wait_ge(x2nT_ready, t + 1)
                sp.dma_start(scratch[bass.ds(t, 1), :, :].rearrange("a p n -> (a p) n"),
                             x2nT[:]).then_inc(stored, 16)

            tiles(sp, lambda i: at(i, 3, store))
            sp.wait_ge(stored, 16 * T)
            def load_xe(t, j):
                sp.dma_start(xe[:, j, :], scratch[bass.ds(t, 1), :, :].rearrange(
                    "a p n -> (a p) n")).then_inc(xe_in[j], 16)

            def store_out(t):
                sp.wait_ge(acc_step, (t + 1) * E)
                sp.dma_start(out[bass.ds(t, 1), :, :].rearrange("a p n -> (a p) n"),
                             h_all[:, bass.ds(t, 1), :].rearrange("p a n -> p (a n)")).then_inc(out_done, 16)

            for j in range(2):
                load_xe(j, j)
            with sp.Fori(0, T // 2 - 1) as i:
                for j in range(2):
                    sp.wait_ge(w1_done, (2 * i + j + 1) * E)
                    load_xe(2 * i + 2 + j, j)
                    store_out(2 * i + j)
            for j in range(2):
                store_out(T - 2 + j)
            sp.wait_ge(out_done, 16 * T)

        @block.gpsimd
        def _(pool):
            pool.memset(half_sb[:], 0.5).then_inc(setup, 1)
            pool.memset(ones_sb[:], 1.0).then_inc(setup, 1)
            pool.memset(vpad[:], 0.0).then_inc(setup, 1)
            pool.memset(kpad[:], 0.0).then_inc(setup, 1)
            pool.memset(qpad[:], 0.0).then_inc(setup, 1)
            pool.iota(iota_sb[:], pattern=[[1, E]], base=0, channel_multiplier=0).then_inc(setup, 1)
            pool.wait_ge(setup, 6)
            pool.wait_ge(tok_fixed, 1)
            pool.wait_ge(consts_in, 16 * len(CONSTS))
            pool.wait_ge(mask_step, 3)

            def load_x(t):
                if later(t):
                    pool.wait_ge(x_ready, t)
                if later(16 * t):
                    pool.wait_ge(rows_in, 16 * t)
                pool.tensor_copy(idx_now[:], tok_sb[:, bass.ds(t, 1)]).then_inc(idx_ready, 1)
                pool.wait_ge(idx_ready, t + 1)
                pool.tensor_tensor(ptick_sb[:], half_sb[:], half_sb[:], ALU.add)
                pool.indirect_dma_start(xg[:], None, emb, bass.IndirectOffsetOnAxis(ap=idx_now[:, 0:1], axis=0)
                                        ).then_inc(rows_in, 16)
                pool.wait_ge(rows_in, 16 * (t + 1))
                if later(t):
                    pool.wait_ge(xT_ps, t)
                if later(t):
                    pool.wait_ge(res_ready, t)
                pool.tensor_tensor(x[:], xg[:], pe_sb[:], ALU.add).then_inc(x_ready, 1)
                pool.wait_ge(x_ready, t + 1)
                pool.tensor_tensor(h_all[:, bass.ds(t, 1), :].rearrange("p a n -> p (a n)"), x[:], row["bo"],
                                   ALU.add).then_inc(res_ready, 1)

            def spread_k(t):
                pool.wait_ge(qk_ready, t + 1)
                if later(t):
                    pool.wait_ge(s_ps, t)
                for c in range(NC):
                    pool.tensor_tensor(kbd[:, c, :, :], qkT[:, NC + c:NC + c + 1, :].broadcast_to([C, HC, P]),
                                       maska_sb[:, :, None].broadcast_to([C, HC, P]),
                                       ALU.mult).then_inc(kbd_ready, 1)

            def spread_k2(t):
                pool.wait_ge(qk2_ready, t + 1)
                if later(t):
                    pool.wait_ge(s2_ps, t)
                for c in range(NC):
                    pool.tensor_tensor(kbd2[:, c, :, :], qk2T[:, NC + c:NC + c + 1, :].broadcast_to([C, HC, P]),
                                       maskb_sb[:, c, :, None].broadcast_to([C, HC, P]),
                                       ALU.mult).then_inc(kbd2_ready, 1)

            def std(t, n):
                pool.wait_ge(var_ready[n], t + 1)
                pool.tensor_tensor(sd[n][:], mv[n][:, 1:2], half_sb[:], ALU.pow).then_inc(std_ready[n], 1)

            def body(i):
                at(i, 1, lambda t: std(t, 0))
                at(i, 3, lambda t: std(t, 3))
                at(i, 0, load_x)
                at(i, 2, spread_k2)
                at(i, 0, spread_k)
                at(i, 1, lambda t: std(t, 1))
                at(i, 1, lambda t: std(t, 2))

            tiles(pool, body)

        @block.tensor
        def _(pe_):
            pe_.wait_ge(consts_in, 16 * len(CONSTS))
            pe_.wait_ge(setup, 6)

            def transpose_pair(dst, src):
                for c in range(NC):
                    mm = pe_.transpose(dst[c], src[:, c * C:(c + 1) * C], id_sb[:])
                return mm

            def project(dst, w, xt):
                for n in range(2):
                    for m in range(NC):
                        for k in range(NC):
                            mm = pe_.matmul(dst[:, (NC * n + m) * P:(NC * n + m + 1) * P],
                                            w[:, n, k, m * C:(m + 1) * C], xt[:, k * P:(k + 1) * P],
                                            start=(k == 0), stop=(k == NC - 1))
                return mm

            def scores(dst, qk, kb):
                for c, h0, n in ((0, 0, 4), (0, 4, 2), (1, 0, 2), (1, 2, 4)):
                    o = (c * HC + h0) * P
                    mm = pe_.matmul(dst[:, o:o + n * P], qk[:, c, :], kb[:, c, h0:h0 + n, :].rearrange(
                        "p h n -> p (h n)"), start=True, stop=True)
                return mm

            def split(ap):
                return [ap[:, c * P:(c + 1) * P] for c in range(NC)]

            def a0_xT(t):
                pe_.wait_ge(x_ready, t + 1)
                if later(t):
                    pe_.wait_ge(pT_lo, t)
                if later(t):
                    pe_.wait_ge(pT_hi, t)
                transpose_pair(split(XT_A), x).then_inc(xT_ps, 1)

            def a1_qkv(t):
                pe_.wait_ge(xT_ready, t + 1)
                project(QK_A, wqkv_sb, xT).then_inc(qk_ps, 1)
                for k in range(NC):
                    mm = pe_.matmul(V_A, xT[:, k * P:(k + 1) * P], wqkv_sb[:, 2, k, :],
                                    start=(k == 0), stop=(k == NC - 1))
                mm.then_inc(v_ps, 1)

            def a2_scores(t):
                pe_.wait_ge(kbd_ready, NC * (t + 1))
                pe_.wait_ge(v_ready, t + 1)
                scores(SA, qkT, kbd).then_inc(s_ps, 1)

            def a3_probT(t):
                pe_.wait_ge(pn_ready, t + 1)
                for h in range(H):
                    mm = pe_.transpose(SA[:, h * P:(h + 1) * P], prob[:, h, :], id_sb[:])
                mm.then_inc(pT_ps, 1)

            def a4_o(t):
                pe_.wait_ge(pT_lo, t + 1)
                pe_.wait_ge(pT_hi, t + 1)
                if later(t):
                    pe_.wait_ge(z_read, t)
                for h in range(H):
                    c, j = divmod(h, HG)
                    mm = pe_.matmul(O_A[G * j:G * j + G, c * P:(c + 1) * P], vpad[:, h, :], probT[:, h, :],
                                    start=True, stop=True)
                mm.then_inc(o_ps, 1)

            def a5_y(t):
                pe_.wait_ge(o_ready, t + 1)
                if later(t):
                    pe_.wait_ge(hid_b, t)
                for c in range(NG):
                    mm = pe_.matmul(Y_A, oT[:, c * P:(c + 1) * P], wo_sb[:, c, :], start=(c == 0), stop=(c == NG - 1))
                mm.then_inc(y_ps, 1)

            def a6_h1T(t):
                pe_.wait_ge(h1_ready, t + 1)
                transpose_pair(split(H1T_A), h1).then_inc(h1T_ps, 1)

            def a7_ff1(t):
                pe_.wait_ge(h1T_ready, t + 1)
                for m in range(FM):
                    o = (m % 3) * P
                    dst = (N0 if m < 3 else N1)[:, o:o + P]
                    for k in range(NC):
                        mm = pe_.matmul(dst, w1_sb[:, k, m * P:(m + 1) * P], h1T[:, k * P:(k + 1) * P],
                                        start=(k == 0), stop=(k == NC - 1))
                    if m == 2:
                        mm.then_inc(fa_ps, 1)
                mm.then_inc(fb_ps, 1)

            def a8_ff2(t):
                pe_.wait_ge(hid_a, t + 1)
                pe_.wait_ge(hid_b, t + 1)
                for m in range(FM):
                    mm = pe_.matmul(Z_A, hid[:, m, :], w2_sb[:, m, :], start=(m == 0), stop=(m == FM - 1))
                mm.then_inc(z_ps, 1)

            def b0_xnT(t):
                pe_.wait_ge(xn_ready, t + 1)
                if later(t):
                    pe_.wait_ge(p2T_lo, t)
                if later(t):
                    pe_.wait_ge(p2T_hi, t)
                if later(t):
                    pe_.wait_ge(u_read, t)
                transpose_pair(split(XNT_B), xn).then_inc(xnT_ps, 1)

            def b1_qk(t):
                pe_.wait_ge(xnT_ready, t + 1)
                project(QK_B, wa_sb, xnT).then_inc(qk2_ps, 1)

            def b2_tok(t):
                pe_.wait_ge(qk2_ready, t + 1)
                if later(t):
                    pe_.wait_ge(aT_ready, t)
                for n in range(2 * NC):
                    mm = pe_.transpose(TOK_B[:, n * C:(n + 1) * C], qk2T[:, n, :], id_sb[0:C, 0:C])
                mm.then_inc(tok_ps, 1)

            def b3_scores(t):
                pe_.wait_ge(kbd2_ready, NC * (t + 1))
                pe_.wait_ge(tok_ready, t + 1)
                if later(t):
                    pe_.wait_ge(x2nT_ready, t)
                if later(t):
                    pe_.wait_ge(lgexp_ready, t)
                scores(SB, qk2T, kbd2).then_inc(s2_ps, 1)

            def b4_probT(t):
                pe_.wait_ge(pn2_ready, t + 1)
                for h in range(H):
                    mm = pe_.transpose(SB[:, h * P:(h + 1) * P], prob2[:, h, :], id_sb[:])
                mm.then_inc(p2T_ps, 1)

            def b5_a(t):
                pe_.wait_ge(p2T_lo, t + 1)
                pe_.wait_ge(p2T_hi, t + 1)
                pe_.wait_ge(tok_ready, t + 1)
                for h in range(H):
                    c, j = divmod(h, HG)
                    dst = A_B[G * j:G * j + G, c * P:(c + 1) * P]
                    pe_.matmul(dst, kpad[:, h, :], prob2T[:, h, :], start=True, stop=False)
                    mm = pe_.matmul(dst, qpad[:, h, :], prob2[:, h, :], start=False, stop=True)
                mm.then_inc(a_ps, 1)

            def b6_u(t):
                pe_.wait_ge(aT_ready, t + 1)
                for c in range(NG):
                    mm = pe_.matmul(U_B, aT[:, c * P:(c + 1) * P], wqk_sb[:, c, :], start=(c == 0), stop=(c == NG - 1))
                mm.then_inc(u_ps, 1)

            def b7_x2nT(t):
                pe_.wait_ge(x2n_ready, t + 1)
                pe_.wait_ge(qk2_ready, min(t + 2, T) if isinstance(t, int) else t + 2)
                transpose_pair(split(X2T_B), x2n).then_inc(x2nT_ps, 1)

            def b8_router(t):
                pe_.wait_ge(x2nT_ready, t + 1)
                for k in range(NC):
                    mm = pe_.matmul(LG_B, x2nT[:, k * P:(k + 1) * P], rw_sb[:, k, :], start=(k == 0), stop=(k == NC - 1))
                mm.then_inc(lg_ps, 1)

            def body(i):
                at(i, 1, a3_probT)
                at(i, 3, b4_probT)
                at(i, 1, a4_o)
                at(i, 3, b5_a)
                at(i, 1, a5_y)
                at(i, 3, b6_u)
                at(i, 0, a0_xT)
                at(i, 2, b0_xnT)
                at(i, 1, a6_h1T)
                at(i, 2, b1_qk)
                at(i, 0, a1_qkv)
                at(i, 3, b7_x2nT)
                at(i, 2, b2_tok)
                at(i, 1, a7_ff1)
                at(i, 3, b8_router)
                at(i, 0, a2_scores)
                at(i, 2, b3_scores)
                at(i, 1, a8_ff2)

            tiles(pe_, body)

            pe_.wait_ge(imp_ready, 1)
            pe_.matmul(SA[:, 0:E], ones_sb[:], imp[:], start=True, stop=True).then_inc(imp_ps, 1)
            pe_.wait_ge(moe_in, 32)
            pe_.wait_ge(comb_ready, 1)

            def experts(i):
                steps = [(j, e) for j in range(2) for e in range(E)]

                def up(n):
                    j, e = steps[n]
                    s = 2 * E * i + n
                    if e == 0:
                        pe_.wait_ge(xe_in[j], 16 * (i + 1))
                    if later(s - 1):
                        pe_.wait_ge(eh_ready, s - 1)
                    for m in range(EM):
                        for k in range(NC):
                            o = e * EI + m * P
                            mm = pe_.matmul(ps[:, e % 2, m * P:(m + 1) * P], m1_sb[:, k, o:o + P],
                                            xe[:, j, k * P:(k + 1) * P], start=(k == 0), stop=(k == NC - 1))
                    mm.then_inc(w1_done, 1)

                def down(n):
                    e = steps[n][1]
                    s = 2 * E * i + n
                    pe_.wait_ge(eh_ready, s + 1)
                    if later(s - 1):
                        pe_.wait_ge(acc_step, s - 1)
                    for m in range(EM):
                        mm = pe_.matmul(ps[:, 2 + e % 2, 0:D], ehid[:, e % 2, m * P:(m + 1) * P], m2_sb[:, m, e, :],
                                        start=(m == 0), stop=(m == EM - 1))
                    mm.then_inc(w2_done, 1)

                up(0)
                for n in range(len(steps)):
                    if n + 1 < len(steps):
                        up(n + 1)
                    down(n)

            pairs(pe_, experts)

        @block.scalar
        def _(act):
            act.wait_ge(consts_in, 16 * len(CONSTS))

            def copy(dst, src):
                return act.activation(dst, src, ACT.Copy)

            def c_xT(t):
                act.wait_ge(xT_ps, t + 1)
                if later(t):
                    act.wait_ge(v_ps, t)
                copy(xT[:], XT_A).then_inc(xT_ready, 1)

            def exponentials(src, dst, nm, ls):
                for h in range(H):
                    a = act.activation(dst[:, h, :], src[:, h * P:(h + 1) * P], ACT.Exp, bias=nm[:, h:h + 1],
                                       accum_out=ls[:, h:h + 1])
                return a

            def c_exp(t):
                if later(t):
                    act.wait_ge(pT_ps, t)
                if later(t):
                    act.wait_ge(r_ready, t)
                act.wait_ge(nm_ready, t + 1)
                exponentials(SA, prob, nmax, lsum).then_inc(p_ready, 1)

            def c_exp2(t):
                if later(t):
                    act.wait_ge(a_ps, t)
                if later(t):
                    act.wait_ge(r2_ready, t)
                act.wait_ge(nm2_ready, t + 1)
                exponentials(SB, prob2, nmax2, lsum2).then_inc(p2_ready, 1)

            def c_pT(t):
                act.wait_ge(pT_ps, t + 1)
                if later(t):
                    act.wait_ge(o_ps, t)
                copy(probT[:, 4:12, :].rearrange("p h n -> p (h n)"), SA[:, 512:1536]).then_inc(pT_hi, 1)

            def c_p2T(t):
                act.wait_ge(p2T_ps, t + 1)
                if later(t):
                    act.wait_ge(a_ps, t)
                copy(prob2T[:, 4:12, :].rearrange("p h n -> p (h n)"), SB[:, 512:1536]).then_inc(p2T_hi, 1)

            def c_o(t):
                act.wait_ge(o_ps, t + 1)
                if later(t):
                    act.wait_ge(y_ps, t)
                copy(oT[:], O_A).then_inc(o_ready, 1)

            def c_h1T(t):
                act.wait_ge(h1T_ps, t + 1)
                if later(t):
                    act.wait_ge(fb_ps, t)
                copy(h1T[:], H1T_A).then_inc(h1T_ready, 1)

            def c_hid(t):
                act.wait_ge(fa_ps, t + 1)
                if later(t):
                    act.wait_ge(z_ps, t)
                for m in range(3):
                    a = act.activation(hid[:, m, :], N0[:, m * P:(m + 1) * P], ACT.Relu, bias=b1_sb[:, m:m + 1])
                a.then_inc(hid_a, 1)

            def c_xnT(t):
                act.wait_ge(xnT_ps, t + 1)
                if later(t):
                    act.wait_ge(qk2_ps, t)
                copy(xnT[:], XNT_B).then_inc(xnT_ready, 1)

            def c_qk2(t):
                act.wait_ge(qk2_ps, t + 1)
                if later(t):
                    act.wait_ge(s2_ps, t)
                copy(qk2T[:].rearrange("p n k -> p (n k)"), QK_B).then_inc(qk2_ready, 1)

            def c_aT(t):
                act.wait_ge(a_ps, t + 1)
                if later(t):
                    act.wait_ge(u_ps, t)
                copy(aT[:], A_B).then_inc(aT_ready, 1)

            def c_lg(t):
                act.wait_ge(lgmax_ready, t + 1)
                if later(t):
                    act.wait_ge(probs_ready, t)
                act.activation(lg[:], LG_B, ACT.Exp, bias=lgmax[:], accum_out=lgsum[:]).then_inc(lgexp_ready, 1)

            def body(i):
                at(i, 1, c_pT)
                at(i, 3, c_p2T)
                at(i, 1, c_o)
                at(i, 3, c_aT)
                at(i, 0, c_xT)
                at(i, 2, c_xnT)
                at(i, 1, c_h1T)
                at(i, 2, c_qk2)
                at(i, 1, c_hid)
                at(i, 3, c_lg)
                at(i, 0, c_exp)
                at(i, 2, c_exp2)

            tiles(act, body)

            def experts(i):
                for n in range(2 * E):
                    s = 2 * E * i + n
                    act.wait_ge(w1_done, s + 1)
                    if later(s - 1):
                        act.wait_ge(w2_done, s - 1)
                    act.activation(ehid[:, n % 2, :], ps[:, n % 2, :], ACT.Silu).then_inc(eh_ready, 1)

            pairs(act, experts)

        @block.vector
        def _(dve):
            dve.wait_ge(tok_in, 16)
            dve.tensor_scalar(neg_sb[:], tok_sb[:], 0.0, float(V), ALU.is_lt, ALU.mult).then_inc(tok_step, 1)
            dve.wait_ge(tok_step, 1)
            dve.tensor_tensor(tok_sb[:], tok_sb[:], neg_sb[:], ALU.add).then_inc(tok_step, 1)
            dve.wait_ge(tok_step, 2)
            dve.tensor_scalar(tok_sb[:], tok_sb[:], 0.0, float(V - 1), ALU.max, ALU.min).then_inc(tok_fixed, 1)
            dve.wait_ge(consts_in, 16 * len(CONSTS))
            dve.wait_ge(setup, 6)
            dve.tensor_scalar(maska_sb[:], mask_sb[:], float(HD) ** -0.5, None, ALU.mult).then_inc(mask_step, 1)
            for c in range(NC):
                dve.tensor_scalar(maskb_sb[:, c, :], mask_sb[:], betas_sb[:, c:c + 1], None,
                                  ALU.mult).then_inc(mask_step, 1)
            dve.tensor_copy(iotaf_sb[:], iota_sb[:]).then_inc(mask_step, 1)
            dve.wait_ge(mask_step, 4)

            ticks = [0]

            def tick():
                k = ticks[0] = (ticks[0] + 1) % 16
                dve.memset(tick_sb[:, k:k + 1], 0.0)

            def hrow(t):
                return h_all[:, bass.ds(t, 1), :].rearrange("p a n -> p (a n)")

            def v_qk(t):
                dve.wait_ge(qk_ps, t + 1)
                if later(t):
                    dve.wait_ge(s_ps, t)
                dve.tensor_tensor(qkT[:], QK_A.rearrange("p (n k) -> p n k", n=2 * NC),
                                  bqk_sb[:, :, None].broadcast_to([C, 2 * NC, P]), ALU.add).then_inc(qk_ready, 1)
                dve.wait_ge(v_ps, t + 1)
                if later(t):
                    dve.wait_ge(o_ps, t)
                dve.tensor_tensor(vpad[:, :, 0:HD], V_A.rearrange("p (h d) -> p h d", h=H),
                                  row["bv"].rearrange("p (h d) -> p h d", h=H), ALU.add).then_inc(v_ready, 1)

            def v_max(t):
                if later(t):
                    dve.wait_ge(p_ready, t)
                dve.wait_ge(s_ps, t + 1)
                dve.tensor_reduce(nmax[:], SA.rearrange("p (h n) -> p h n", h=H), AX.X, ALU.max,
                                  negate=True).then_inc(nm_ready, 1)

            def v_max2(t):
                if later(t):
                    dve.wait_ge(p2_ready, t)
                dve.wait_ge(s2_ps, t + 1)
                dve.tensor_reduce(nmax2[:], SB.rearrange("p (h n) -> p h n", h=H), AX.X, ALU.max,
                                  negate=True).then_inc(nm2_ready, 1)

            def v_norm(t):
                if later(t):
                    dve.wait_ge(pn_ready, t)
                dve.wait_ge(p_ready, t + 1)
                dve.reciprocal(rsum[:], lsum[:]).then_inc(r_ready, 1)
                dve.wait_ge(r_ready, t + 1)
                dve.tensor_tensor(prob[:], prob[:], rsum[:, :, None].broadcast_to([P, H, P]),
                                  ALU.mult).then_inc(pn_ready, 1)

            def v_norm2(t):
                if later(t):
                    dve.wait_ge(pn2_ready, t)
                dve.wait_ge(p2_ready, t + 1)
                dve.reciprocal(rsum2[:], lsum2[:]).then_inc(r2_ready, 1)
                dve.wait_ge(r2_ready, t + 1)
                dve.tensor_tensor(prob2[:], prob2[:], rsum2[:, :, None].broadcast_to([P, H, P]),
                                  ALU.mult).then_inc(pn2_ready, 1)

            def v_pT(t):
                dve.wait_ge(pT_ps, t + 1)
                if later(t):
                    dve.wait_ge(o_ps, t)
                dve.tensor_copy(probT[:, 0:4, :].rearrange("p h n -> p (h n)"), SA[:, 0:512]).then_inc(pT_lo, 1)

            def v_p2T(t):
                dve.wait_ge(p2T_ps, t + 1)
                if later(t):
                    dve.wait_ge(a_ps, t)
                dve.tensor_copy(prob2T[:, 0:4, :].rearrange("p h n -> p (h n)"), SB[:, 0:512]).then_inc(p2T_lo, 1)

            def v_hid(t):
                dve.wait_ge(fb_ps, t + 1)
                if later(t):
                    dve.wait_ge(z_ps, t)
                for m in range(3, FM):
                    v = dve.tensor_scalar(hid[:, m, :], N1[:, (m - 3) * P:(m - 2) * P], b1_sb[:, m:m + 1], 0.0,
                                          ALU.add, ALU.max)
                v.then_inc(hid_b, 1)

            def stats(n, t, src, eps):
                tick()
                dve.bn_stats(st[n][:], src).then_inc(st_ready[n], 1)
                dve.wait_ge(st_ready[n], t + 1)
                tick()
                dve.bn_aggr(mv[n][:], st[n][:]).then_inc(mv_ready[n], 1)
                dve.wait_ge(mv_ready[n], t + 1)
                dve.tensor_scalar(mv[n][:, 1:2], mv[n][:, 1:2], eps, None, ALU.add).then_inc(var_ready[n], 1)

            def tok_norm(n, t, src, tmp, gamma, beta):
                dve.wait_ge(std_ready[n], t + 1)
                dve.tensor_scalar(sd[n][:], sd[n][:], EPS_TOK, None, ALU.add).then_inc(sd_ready[n], 1)
                dve.wait_ge(sd_ready[n], t + 1)
                dve.reciprocal(rstd[n][:], sd[n][:]).then_inc(rstd_ready[n], 1)
                dve.wait_ge(rstd_ready[n], t + 1)
                dve.tensor_scalar(tmp, src, mv[n][:, 0:1], rstd[n][:], ALU.subtract, ALU.mult).then_inc(centred[n], 1)
                dve.wait_ge(centred[n], t + 1)
                dve.tensor_tensor(tmp, tmp, gamma, ALU.mult).then_inc(scaled[n], 1)
                dve.wait_ge(scaled[n], t + 1)

            def v_y(t):
                dve.wait_ge(y_ps, t + 1)
                dve.wait_ge(res_ready, t + 1)
                dve.tensor_tensor(y[:], Y_A, hrow(t), ALU.add).then_inc(y_read, 1)
                dve.wait_ge(y_read, t + 1)
                stats(0, t, y[:], 0.0)
                tok_norm(0, t, y[:], y[:], row["gamma1"], row["beta1"])
                if later(t):
                    dve.wait_ge(h1T_ps, t)
                dve.tensor_tensor(h1[:], y[:], row["beta1"], ALU.add).then_inc(h1_ready, 1)

            def v_z(t):
                dve.wait_ge(z_ps, t + 1)
                dve.wait_ge(h1_ready, t + 1)
                dve.tensor_tensor(z[:], Z_A, h1[:], ALU.add).then_inc(z_read, 1)
                dve.wait_ge(z_read, t + 1)
                dve.tensor_tensor(z[:], z[:], row["b2"], ALU.add).then_inc(z_ready, 1)
                dve.wait_ge(z_ready, t + 1)
                stats(1, t, z[:], 0.0)
                tok_norm(1, t, z[:], z[:], row["gamma2"], row["beta2"])
                dve.tensor_tensor(hs[:], z[:], row["beta2"], ALU.add).then_inc(hs_ready, 1)
                dve.wait_ge(hs_ready, t + 1)
                tick()
                dve.tensor_copy(hrow(t), hs[:]).then_inc(h_ready, 1)
                stats(2, t, hs[:], EPS_LN)
                dve.wait_ge(std_ready[2], t + 1)
                dve.reciprocal(rstd[2][:], sd[2][:]).then_inc(rstd_ready[2], 1)
                dve.wait_ge(rstd_ready[2], t + 1)
                if later(t):
                    dve.wait_ge(xnT_ps, t)
                dve.tensor_scalar(xn[:], hs[:], mv[2][:, 0:1], rstd[2][:], ALU.subtract,
                                  ALU.mult).then_inc(xn_ready, 1)

            def v_tok(t):
                dve.wait_ge(tok_ps, t + 1)
                if later(t):
                    dve.wait_ge(a_ps, t)
                dve.tensor_copy(qpad[:, :, HD:G], TOK_B[:, 0:D].rearrange("p (h d) -> p h d", h=H))
                dve.tensor_copy(kpad[:, :, 0:HD], TOK_B[:, D:2 * D].rearrange("p (h d) -> p h d", h=H)
                                ).then_inc(tok_ready, 1)

            def v_u(t):
                dve.wait_ge(u_ps, t + 1)
                dve.wait_ge(xn_ready, t + 1)
                dve.tensor_tensor(h2[:], U_B, hrow(t), ALU.add).then_inc(u_read, 1)
                dve.wait_ge(u_read, t + 1)
                tick()
                dve.tensor_copy(hrow(t), h2[:])
                stats(3, t, h2[:], EPS_LN)
                dve.wait_ge(std_ready[3], t + 1)
                dve.reciprocal(rstd[3][:], sd[3][:]).then_inc(rstd_ready[3], 1)
                dve.wait_ge(rstd_ready[3], t + 1)
                if later(t):
                    dve.wait_ge(x2nT_ps, t)
                dve.tensor_scalar(x2n[:], h2[:], mv[3][:, 0:1], rstd[3][:], ALU.subtract,
                                  ALU.mult).then_inc(x2n_ready, 1)

            def v_x2nT(t):
                dve.wait_ge(x2nT_ps, t + 1)
                if later(t):
                    dve.wait_ge(lg_ps, t)
                if later(16 * t):
                    dve.wait_ge(stored, 16 * t)
                dve.tensor_copy(x2nT[:], X2T_B).then_inc(x2nT_ready, 1)

            def v_lgmax(t):
                dve.wait_ge(lg_ps, t + 1)
                dve.tensor_reduce(lgmax[:], LG_B, AX.X, ALU.max, negate=True).then_inc(lgmax_ready, 1)

            def v_probs(t):
                dve.wait_ge(lgexp_ready, t + 1)
                dve.reciprocal(lginv[:], lgsum[:]).then_inc(lginv_ready, 1)
                dve.wait_ge(lginv_ready, t + 1)
                dve.tensor_scalar(pr[:], lg[:], lginv[:], None, ALU.mult).then_inc(pr_ready, 1)
                dve.wait_ge(pr_ready, t + 1)
                tick()
                dve.tensor_copy(probs_all[:, bass.ds(t, 1), :].rearrange("p a e -> p (a e)"), pr[:])
                dve.max(top8[:], pr[:]).then_inc(top8_ready, 1)
                dve.wait_ge(top8_ready, t + 1)
                tick()
                dve.max_index(idx8[:], top8[:], pr[:]).then_inc(idx8_ready, 1)
                dve.wait_ge(idx8_ready, t + 1)
                tick()
                dve.tensor_copy(idx_all[:, bass.ds(t, 1), :].rearrange("p a e -> p (a e)"),
                                idx8[:, 0:2]).then_inc(probs_ready, 1)

            def body(i):
                at(i, 1, v_pT)
                at(i, 3, v_p2T)
                at(i, 1, v_y)
                at(i, 3, v_u)
                at(i, 0, v_qk)
                at(i, 3, v_x2nT)
                at(i, 2, v_tok)
                at(i, 3, v_lgmax)
                at(i, 1, v_hid)
                at(i, 0, v_max)
                at(i, 2, v_max2)
                at(i, 3, v_probs)
                at(i, 0, v_norm)
                at(i, 1, v_z)
                at(i, 2, v_norm2)

            tiles(dve, body)

            dve.wait_ge(probs_ready, T)
            dve.tensor_reduce(imp[:], probs_all[:].rearrange("p t e -> p e t"), AX.X, ALU.add).then_inc(imp_ready, 1)
            dve.tensor_copy(idxf[:], idx_all[:]).then_inc(comb_step, 1)
            dve.wait_ge(comb_step, 1)
            iota_b = iotaf_sb[:, None, :].broadcast_to([P, T, E])
            dve.tensor_tensor(one1[:], idxf[:, :, 0:1].broadcast_to([P, T, E]), iota_b, ALU.is_equal).then_inc(comb_step, 1)
            dve.wait_ge(comb_step, 2)
            dve.tensor_tensor(one2[:], idxf[:, :, 1:2].broadcast_to([P, T, E]), iota_b, ALU.is_equal).then_inc(comb_step, 1)
            dve.wait_ge(comb_step, 3)
            dve.tensor_tensor(one1[:], one1[:], one2[:], ALU.add).then_inc(comb_step, 1)
            dve.wait_ge(comb_step, 4)
            dve.wait_ge(imp_ps, 1)
            dve.tensor_scalar(rinv[:], SA[:, 0:E], -1.0, 1.0 - 0.9, ALU.add, ALU.mult).then_inc(comb_step, 1)
            dve.wait_ge(comb_step, 5)
            dve.tensor_scalar(rinv[:], rinv[:], 1.0, 0.01, ALU.add, ALU.add).then_inc(comb_step, 1)
            dve.wait_ge(comb_step, 6)
            dve.reciprocal(rinv[:], rinv[:]).then_inc(comb_step, 1)
            dve.wait_ge(comb_step, 7)
            dve.tensor_tensor(comb[:], probs_all[:], rinv[:, None, :].broadcast_to([P, T, E]), ALU.mult).then_inc(comb_step, 1)
            dve.wait_ge(comb_step, 8)
            dve.tensor_tensor(comb[:], comb[:], one1[:], ALU.mult).then_inc(comb_step, 1)
            dve.wait_ge(comb_step, 9)
            dve.tensor_reduce(csum[:], comb[:], AX.X, ALU.add).then_inc(comb_step, 1)
            dve.wait_ge(comb_step, 10)
            dve.reciprocal(csum[:], csum[:]).then_inc(comb_step, 1)
            dve.wait_ge(comb_step, 11)
            dve.tensor_tensor(comb[:], comb[:], csum[:, :, None].broadcast_to([P, T, E]),
                              ALU.mult).then_inc(comb_ready, 1)
            dve.wait_ge(comb_ready, 1)
            def experts(i):
                for j in range(2):
                    t = 2 * i + j
                    for e in range(E):
                        s = t * E + e
                        dve.wait_ge(w2_done, s + 1)
                        if later(s):
                            dve.wait_ge(acc_step, s)
                        cw = comb[:, bass.ds(t, 1), e:e + 1].rearrange("p a n -> p (a n)")
                        dve.scalar_tensor_tensor(hrow(t), ps[:, 2 + e % 2, 0:D], cw, hrow(t), ALU.mult,
                                                 ALU.add).then_inc(acc_step, 1)

            pairs(dve, experts)


def position_table():
    import numpy as np
    pos = np.arange(P, dtype=np.float32)[:, None]
    i = np.arange(D, dtype=np.float32)[None, :]
    ang = pos / np.power(np.float32(10000.0), np.float32(2.0) * i / np.float32(D))
    return np.where((np.arange(D) % 2 == 0)[None, :], np.cos(ang), np.sin(ang)).astype(np.float32)


def lay_out(a):
    import numpy as np

    def chunks(w, rows):
        return w.reshape(w.shape[0] // rows, rows, -1).transpose(1, 0, 2)

    def heads(first, second):
        w = np.zeros((H, 2, HD, D), np.float32)
        w[:, 0] = first.reshape(H, HD, D)
        if second is not None:
            w[:, 1] = second.reshape(H, HD, D)
        return chunks(w.reshape(H * G, D), P)

    row_names = [a["L0_tok_" + n] for n in ROWS]
    return {
        "tok": a["x"].T,
        "emb": a["L0_tok_emb"],
        "pe": position_table(),
        "ident": np.eye(P, dtype=np.float32),
        "hmask": (np.arange(C)[:, None] // HD == np.arange(HC)[None, :]).astype(np.float32),
        "w_qkv": np.stack([chunks(a["L0_tok_" + n], C) for n in ("wq", "wk", "wv")], 1),
        "bqk": np.concatenate([a["L0_tok_bq"].reshape(NC, C), a["L0_tok_bk"].reshape(NC, C)]).T,
        "rows": np.broadcast_to(np.stack(row_names)[None], (P, len(ROWS), D)),
        "wo": heads(a["L0_tok_wo"], None),
        "w1": chunks(a["L0_tok_w1"], C),
        "b1": a["L0_tok_b1"].reshape(FM, P).T,
        "w2": chunks(a["L0_tok_w2"], P),
        "wa": np.stack([chunks(a["L0_attn_Wq"].T, C), chunks(a["L0_attn_Wk"].T, C)], 1),
        "betas": np.repeat(a["L0_attn_betas"], HD).reshape(NC, C).T,
        "wqk": heads(a["L0_attn_Wq"], a["L0_attn_Wk"]),
        "rw": chunks(a["L0_ffn_router_w"].T, C),
        "m1": chunks(a["L0_ffn_w1"].transpose(2, 0, 1).reshape(D, E * EI), C),
        "m2": a["L0_ffn_w2"].transpose(2, 0, 1).reshape(EM, P, E, D).transpose(1, 0, 2, 3),
    }


def kernel(**inputs):
    import numpy as np
    import concourse.bacc as bacc
    from concourse.bass_utils import run_bass_kernel_spmd

    nc = bacc.Bacc("TRN2", target_bir_lowering=False, num_devices=1)
    arrays, args = {}, {}
    for name, a in lay_out({k: np.asarray(v) for k, v in inputs.items()}).items():
        arrays[f"in_{name}"] = np.ascontiguousarray(a)
        args[name] = nc.dram_tensor(f"in_{name}", a.shape, mybir.dt.from_np(a.dtype), kind="ExternalInput").ap()
    out = nc.dram_tensor("out", (T, P, D), F32, kind="ExternalOutput").ap()
    scratch = nc.dram_tensor("scratch", (T, C, NC * P), F32, kind="Internal").ap()
    tower_kernel(nc, out=out, scratch=scratch, **args)
    r = run_bass_kernel_spmd(nc, [arrays], core_ids=[0])
    return r.results[0]["out"]
```

```python
from contextlib import ExitStack

import concourse.bass as bass
from concourse import mybir

ALU = mybir.AluOpType
ACT = mybir.ActivationFunctionType
AX = mybir.AxisListType
F32 = mybir.dt.float32
I32 = mybir.dt.int32
U32 = mybir.dt.uint32

P = 128
T = 64
D = 192
C = 96
NC = D // C
H = 12
HD = D // H
HC = C // HD
G = 32
HG = P // G
NG = H // HG
FF = 768
FM = FF // P
V = 8000
E = 8
EI = 512
EM = EI // P
EPS_TOK = 1e-05
EPS_LN = 1e-05
ROWS = ("bv", "bo", "b2", "gamma1", "beta1", "gamma2", "beta2")
SKEW = 5


def tower_kernel(nc, tok, emb, pe, ident, hmask, w_qkv, bqk, rows, wo, w1, b1, w2, wa, betas, wqk,
                 rw, m1, m2, out, scratch):
    ctx = ExitStack()
    with ctx:
        def sb(name, shape, dt=F32):
            return ctx.enter_context(nc.sbuf_tensor(name, shape, dt))

        def sem(name):
            return ctx.enter_context(nc.semaphore(name))

        tok_sb = sb("tok_sb", [P, T], I32)
        neg_sb = sb("neg_sb", [P, T], I32)
        pe_sb = sb("pe_sb", [P, D])
        id_sb = sb("id_sb", [P, P])
        mask_sb = sb("mask_sb", [C, HC])
        maska_sb = sb("maska_sb", [C, HC])
        maskb_sb = sb("maskb_sb", [C, NC, HC])
        betas_sb = sb("betas_sb", [C, NC])
        wqkv_sb = sb("wqkv_sb", [C, 3, NC, D])
        bqk_sb = sb("bqk_sb", [C, 2 * NC])
        rows_sb = sb("rows_sb", [P, len(ROWS), D])
        wo_sb = sb("wo_sb", [P, NG, D])
        w1_sb = sb("w1_sb", [C, NC, FF])
        b1_sb = sb("b1_sb", [P, FM])
        w2_sb = sb("w2_sb", [P, FM, D])
        wa_sb = sb("wa_sb", [C, 2, NC, D])
        wqk_sb = sb("wqk_sb", [P, NG, D])
        rw_sb = sb("rw_sb", [C, NC, E])
        m1_sb = sb("m1_sb", [C, NC, E * EI])
        m2_sb = sb("m2_sb", [P, EM, E, D])
        half_sb = sb("half_sb", [P, 1])
        mhalf_sb = sb("mhalf_sb", [P, 1])
        eps_sb = sb("eps_sb", [P, 1])
        tick_sb = sb("tick_sb", [P, 16])
        ptick_sb = sb("ptick_sb", [P, 1])
        ones_sb = sb("ones_sb", [P, P])
        iota_sb = sb("iota_sb", [P, E], U32)
        iotaf_sb = sb("iotaf_sb", [P, E])
        row = {name: rows_sb[:, i, :] for i, name in enumerate(ROWS)}

        h_all = sb("h_all", [P, T, D])
        probs_all = sb("probs_all", [P, T, E])
        idx_all = sb("idx_all", [P, T, 2], U32)

        idx_now = sb("idx_now", [P, 1], U32)
        xg = sb("xg", [P, D])
        x = sb("x", [P, D])
        xT = sb("xT", [C, NC * P])
        qkT = sb("qkT", [C, 2 * NC, P])
        kbd = sb("kbd", [C, NC, HC, P])
        vpad = sb("vpad", [P, H, G])
        prob = sb("prob", [P, H, P])
        probT = sb("probT", [P, H, P])
        nmax = sb("nmax", [P, H])
        lsum = sb("lsum", [P, H])
        rsum = sb("rsum", [P, H])
        oT = sb("oT", [P, NG * P])
        y = sb("y", [P, D])
        h1 = sb("h1", [P, D])
        h1T = sb("h1T", [C, NC * P])
        hid = sb("hid", [P, FM, P])
        z = sb("z", [P, D])
        yc = sb("yc", [P, D])
        zc = sb("zc", [P, D])
        hs = sb("hs", [P, D])
        h2 = sb("h2", [P, D])
        xn = sb("xn", [P, D])
        xnT = sb("xnT", [C, NC * P])
        qk2T = sb("qk2T", [C, 2 * NC, P])
        kbd2 = sb("kbd2", [C, NC, HC, P])
        kpad = sb("kpad", [P, H, G])
        qpad = sb("qpad", [P, H, G])
        prob2 = sb("prob2", [P, H, P])
        prob2T = sb("prob2T", [P, H, P])
        nmax2 = sb("nmax2", [P, H])
        lsum2 = sb("lsum2", [P, H])
        rsum2 = sb("rsum2", [P, H])
        aT = sb("aT", [P, NG * P])
        x2n = sb("x2n", [P, D])
        x2nT = sb("x2nT", [C, NC * P])
        lg = sb("lg", [P, 8])
        lgmax = sb("lgmax", [P, 1])
        lgsum = sb("lgsum", [P, 1])
        lginv = sb("lginv", [P, 1])
        pr = sb("pr", [P, E])
        top8 = sb("top8", [P, 8])
        idx8 = sb("idx8", [P, 8], U32)
        st = [sb(f"st{i}", [P, 6]) for i in range(4)]
        mv = [sb(f"mv{i}", [P, 2]) for i in range(4)]
        sd = [sb(f"sd{i}", [P, 1]) for i in range(4)]
        rstd = [sb(f"rstd{i}", [P, 1]) for i in range(4)]

        idxf = sb("idxf", [P, T, 2])
        imp = sb("imp", [P, E])
        rinv = sb("rinv", [P, E])
        one1 = probT[:, 0:4, :].rearrange("p h n -> p (h n)").rearrange("p (t e) -> p t e", e=E)
        one2 = probT[:, 4:8, :].rearrange("p h n -> p (h n)").rearrange("p (t e) -> p t e", e=E)
        csum = sb("csum", [P, T])
        comb = sb("comb", [P, T, E])
        xe = kbd[:, 0, 0:4, :].rearrange("p (s c) n -> p s (c n)", s=2)
        ehid = prob[:, 0:8, :].rearrange("p (s m) n -> p s (m n)", s=2)

        ps = ctx.enter_context(nc.psum_tensor("ps", [P, 8, 512], F32))
        flat = ps[:, :, :].rearrange("p b n -> p (b n)")
        SA = flat[:, 0:1536]
        SB = flat[:, 1536:3072]
        N0 = flat[:, 3072:3584]
        N1 = flat[:, 3584:4096]
        QK_A = SA[0:C, 0:512]
        V_A = SA[:, 512:704]
        XT_A = SA[0:C, 1024:1280]
        O_A = N0[:, 0:384]
        Y_A = N1[:, 0:192]
        H1T_A = N1[0:C, 192:448]
        Z_A = N0[:, 0:192]
        XNT_B = SB[0:C, 1280:1536]
        QK_B = SB[0:C, 0:512]
        TOK_B = SB[:, 512:896]
        A_B = SB[:, 512:896]
        U_B = SB[:, 1024:1216]
        X2T_B = N1[0:C, 0:256]
        LG_B = N0[:, 256:264]

        tok_in = sem("tok_in")
        consts_in = sem("consts_in")
        moe_in = sem("moe_in")
        setup = sem("setup")
        tok_step = sem("tok_step")
        tok_fixed = sem("tok_fixed")
        mask_step = sem("mask_step")
        idx_ready = sem("idx_ready")
        rows_in = sem("rows_in")
        x_ready = sem("x_ready")
        res_ready = sem("res_ready")
        xT_ps = sem("xT_ps")
        xT_ready = sem("xT_ready")
        qk_ps = sem("qk_ps")
        v_ps = sem("v_ps")
        qk_ready = sem("qk_ready")
        v_ready = sem("v_ready")
        kbd_ready = sem("kbd_ready")
        s_lo = sem("s_lo")
        s_ps = sem("s_ps")
        nm_lo = sem("nm_lo")
        p_lo = sem("p_lo")
        r_lo = sem("r_lo")
        nm_ready = sem("nm_ready")
        p_ready = sem("p_ready")
        r_ready = sem("r_ready")
        pn_lo = sem("pn_lo")
        pn_hi = sem("pn_hi")
        pT_bank0 = sem("pT_bank0")
        pT_ps = sem("pT_ps")
        pT_lo = sem("pT_lo")
        pT_hi = sem("pT_hi")
        o_ps = sem("o_ps")
        o_ready = sem("o_ready")
        y_ps = sem("y_ps")
        y_read = sem("y_read")
        h1_ready = sem("h1_ready")
        h1T_ps = sem("h1T_ps")
        h1T_ready = sem("h1T_ready")
        fa_ps = sem("fa_ps")
        fb_ps = sem("fb_ps")
        hid_a = sem("hid_a")
        hid_b = sem("hid_b")
        z_ps = sem("z_ps")
        z_read = sem("z_read")
        z_ready = sem("z_ready")
        hs_ready = sem("hs_ready")
        h_ready = sem("h_ready")
        h1b_ready = sem("h1b_ready")
        xn_ready = sem("xn_ready")
        xnT_ps = sem("xnT_ps")
        xnT_ready = sem("xnT_ready")
        qk2_ps = sem("qk2_ps")
        qk2_ready = sem("qk2_ready")
        kbd2_ready = sem("kbd2_ready")
        kbd2_hi = sem("kbd2_hi")
        tok_ps = sem("tok_ps")
        tok_ready = sem("tok_ready")
        s2_lo = sem("s2_lo")
        s2_ps = sem("s2_ps")
        nm2_lo = sem("nm2_lo")
        p2_lo = sem("p2_lo")
        r2_lo = sem("r2_lo")
        nm2_ready = sem("nm2_ready")
        p2_ready = sem("p2_ready")
        r2_ready = sem("r2_ready")
        pn2_lo = sem("pn2_lo")
        pn2_hi = sem("pn2_hi")
        p2T_bank0 = sem("p2T_bank0")
        p2T_ps = sem("p2T_ps")
        p2T_lo = sem("p2T_lo")
        p2T_hi = sem("p2T_hi")
        a_ps = sem("a_ps")
        aT_ready = sem("aT_ready")
        u_ps = sem("u_ps")
        u_read = sem("u_read")
        x2n_ready = sem("x2n_ready")
        x2nT_ps = sem("x2nT_ps")
        x2nT_ready = sem("x2nT_ready")
        stored = sem("stored")
        lg_ps = sem("lg_ps")
        lgmax_ready = sem("lgmax_ready")
        lgexp_ready = sem("lgexp_ready")
        lginv_ready = sem("lginv_ready")
        pr_ready = sem("pr_ready")
        top8_ready = sem("top8_ready")
        idx8_ready = sem("idx8_ready")
        probs_ready = sem("probs_ready")
        imp_ready = sem("imp_ready")
        imp_ps = sem("imp_ps")
        comb_step = sem("comb_step")
        comb_ready = sem("comb_ready")
        w1_done = sem("w1_done")
        eh_ready = sem("eh_ready")
        w2_done = sem("w2_done")
        acc_step = sem("acc_step")
        out_done = sem("out_done")
        xe_in = [sem(f"xe_in{j}") for j in range(2)]
        st_ready = [sem(f"st_ready{n}") for n in range(4)]
        mv_ready = [sem(f"mv_ready{n}") for n in range(4)]
        shifted = [sem(f"shifted{n}") for n in range(4)]
        var_ready = [sem(f"var_ready{n}") for n in range(4)]
        std_ready = [sem(f"std_ready{n}") for n in range(4)]
        sd_ready = [sem(f"sd_ready{n}") for n in range(4)]
        rstd_ready = [sem(f"rstd_ready{n}") for n in range(4)]
        centred = [sem(f"centred{n}") for n in range(4)]
        scaled = [sem(f"scaled{n}") for n in range(4)]

        def later(n):
            return not isinstance(n, int) or n > 0

        def tiles(eng, body):
            for i in range(SKEW + 1):
                body(i)
            with eng.Fori(SKEW + 1, T - 1) as i:
                body(i)
            for i in range(T - 1, T + SKEW):
                body(i)

        def upto(n):
            return min(n, T) if isinstance(n, int) else n

        def pairs(eng, body):
            body(0)
            with eng.Fori(1, T // 2) as i:
                body(i)

        def at(i, skew, stage):
            t = i - skew
            if isinstance(i, int) and not 0 <= t < T:
                return
            stage(t)

        def hrow(t):
            return h_all[:, bass.ds(t, 1), :].rearrange("p a n -> p (a n)")

        block = ctx.enter_context(nc.Block())

        CONSTS = [(pe_sb[:], pe), (id_sb[:], ident), (mask_sb[:], hmask), (wqkv_sb[:], w_qkv),
                  (bqk_sb[:], bqk), (rows_sb[:], rows), (wo_sb[:], wo), (w1_sb[:], w1), (b1_sb[:], b1),
                  (w2_sb[:], w2), (wa_sb[:], wa), (betas_sb[:], betas), (wqk_sb[:], wqk), (rw_sb[:], rw)]

        @block.sync
        def _(sp):
            sp.dma_start(tok_sb[:], tok).then_inc(tok_in, 16)
            for dst, src in CONSTS:
                sp.dma_start(dst, src).then_inc(consts_in, 16)
            sp.dma_start(m1_sb[:], m1).then_inc(moe_in, 16)
            sp.dma_start(m2_sb[:], m2).then_inc(moe_in, 16)

            def store(t):
                sp.wait_ge(x2nT_ready, t + 1)
                sp.dma_start(scratch[bass.ds(t, 1), :, :].rearrange("a p n -> (a p) n"),
                             x2nT[:]).then_inc(stored, 16)

            tiles(sp, lambda i: at(i, 5, store))
            sp.wait_ge(stored, 16 * T)
            def load_xe(t, j):
                sp.dma_start(xe[:, j, :], scratch[bass.ds(t, 1), :, :].rearrange(
                    "a p n -> (a p) n")).then_inc(xe_in[j], 16)

            def store_out(t):
                sp.wait_ge(acc_step, (t + 1) * E)
                sp.dma_start(out[bass.ds(t, 1), :, :].rearrange("a p n -> (a p) n"),
                             h_all[:, bass.ds(t, 1), :].rearrange("p a n -> p (a n)")).then_inc(out_done, 16)

            for j in range(2):
                load_xe(j, j)
            with sp.Fori(0, T // 2 - 1) as i:
                for j in range(2):
                    sp.wait_ge(w1_done, (2 * i + j + 1) * E)
                    load_xe(2 * i + 2 + j, j)
                    store_out(2 * i + j)
            for j in range(2):
                store_out(T - 2 + j)
            sp.wait_ge(out_done, 16 * T)

        @block.gpsimd
        def _(pool):
            pool.memset(half_sb[:], 0.5).then_inc(setup, 1)
            pool.memset(mhalf_sb[:], -0.5).then_inc(setup, 1)
            pool.memset(eps_sb[:], EPS_LN).then_inc(setup, 1)
            pool.memset(ones_sb[:], 1.0).then_inc(setup, 1)
            pool.memset(vpad[:], 0.0).then_inc(setup, 1)
            pool.memset(kpad[:], 0.0).then_inc(setup, 1)
            pool.memset(qpad[:], 0.0).then_inc(setup, 1)
            pool.iota(iota_sb[:], pattern=[[1, E]], base=0, channel_multiplier=0).then_inc(setup, 1)
            pool.wait_ge(setup, 8)
            pool.wait_ge(tok_fixed, 1)
            pool.wait_ge(consts_in, 16 * len(CONSTS))
            pool.wait_ge(mask_step, 3)

            def gather(t):
                if later(t):
                    pool.wait_ge(rows_in, 16 * t)
                    pool.wait_ge(x_ready, t)
                pool.tensor_copy(idx_now[:], tok_sb[:, bass.ds(t, 1)]).then_inc(idx_ready, 1)
                pool.wait_ge(idx_ready, t + 1)
                pool.tensor_tensor(ptick_sb[:], half_sb[:], half_sb[:], ALU.add)
                pool.indirect_dma_start(xg[:], None, emb, bass.IndirectOffsetOnAxis(ap=idx_now[:, 0:1], axis=0)
                                        ).then_inc(rows_in, 16)

            def embed(t):
                pool.wait_ge(rows_in, 16 * (t + 1))
                if later(t):
                    pool.wait_ge(xT_ps, t)
                    pool.wait_ge(res_ready, t)
                pool.tensor_tensor(x[:], xg[:], pe_sb[:], ALU.add).then_inc(x_ready, 1)
                pool.wait_ge(x_ready, t + 1)
                pool.tensor_tensor(hrow(t), x[:], row["bo"], ALU.add).then_inc(res_ready, 1)

            def spread_k(t):
                pool.wait_ge(qk_ready, t + 1)
                if later(t):
                    pool.wait_ge(s_ps, t)
                for c in range(NC):
                    pool.tensor_tensor(kbd[:, c, :, :], qkT[:, NC + c:NC + c + 1, :].broadcast_to([C, HC, P]),
                                       maska_sb[:, :, None].broadcast_to([C, HC, P]),
                                       ALU.mult).then_inc(kbd_ready, 1)

            def spread_k2(t):
                pool.wait_ge(qk2_ready, t + 1)
                if later(t):
                    pool.wait_ge(s2_ps, t)
                pool.tensor_tensor(kbd2[:, 0, :, :], qk2T[:, NC:NC + 1, :].broadcast_to([C, HC, P]),
                                   maskb_sb[:, 0, :, None].broadcast_to([C, HC, P]), ALU.mult).then_inc(kbd2_ready, 1)

            def std_tok(t, n):
                pool.wait_ge(mv_ready[n], t + 1)
                pool.tensor_tensor(sd[n][:], mv[n][:, 1:2], half_sb[:], ALU.pow).then_inc(std_ready[n], 1)

            def rstd_plain(t, n):
                pool.wait_ge(mv_ready[n], t + 1)
                if later(t):
                    pool.wait_ge(std_ready[n], t)
                pool.tensor_tensor(sd[n][:], mv[n][:, 1:2], eps_sb[:], ALU.add).then_inc(var_ready[n], 1)
                pool.wait_ge(var_ready[n], t + 1)
                pool.tensor_tensor(rstd[n][:], sd[n][:], mhalf_sb[:], ALU.pow).then_inc(std_ready[n], 1)

            def residual1(t):
                pool.wait_ge(h1_ready, t + 1)
                pool.tensor_tensor(hrow(t), h1[:], row["b2"], ALU.add).then_inc(h1b_ready, 1)

            def norm_hi(t):
                pool.wait_ge(r_ready, t + 1)
                pool.tensor_tensor(prob[:, 8:12, :], prob[:, 8:12, :], rsum[:, 8:12, None].broadcast_to([P, 4, P]),
                                   ALU.mult).then_inc(pn_hi, 1)

            def norm2_hi(t):
                pool.wait_ge(r2_ready, t + 1)
                pool.tensor_tensor(prob2[:, 8:12, :], prob2[:, 8:12, :], rsum2[:, 8:12, None].broadcast_to([P, 4, P]),
                                   ALU.mult).then_inc(pn2_hi, 1)

            def body(i):
                at(i, 0, embed)
                at(i, -1, gather)
                at(i, 1, lambda t: std_tok(t, 0))
                at(i, 3, lambda t: std_tok(t, 1))
                at(i, 0, spread_k)
                at(i, 3, lambda t: rstd_plain(t, 2))
                at(i, 1, residual1)
                at(i, 4, norm2_hi)
                at(i, 3, spread_k2)
                at(i, 4, lambda t: rstd_plain(t, 3))
                at(i, 0, norm_hi)

            gather(0)
            tiles(pool, body)

        @block.tensor
        def _(pe_):
            pe_.wait_ge(consts_in, 16 * len(CONSTS))
            pe_.wait_ge(setup, 8)

            def transpose_pair(dst, src):
                for c in range(NC):
                    mm = pe_.transpose(dst[c], src[:, c * C:(c + 1) * C], id_sb[:])
                return mm

            def project(dst, w, xt):
                for n in range(2):
                    for m in range(NC):
                        for k in range(NC):
                            mm = pe_.matmul(dst[:, (NC * n + m) * P:(NC * n + m + 1) * P],
                                            w[:, n, k, m * C:(m + 1) * C], xt[:, k * P:(k + 1) * P],
                                            start=(k == 0), stop=(k == NC - 1))
                return mm

            def scores(dst, qk, kb, first_bank):
                for c, h0, n in ((0, 0, 4), (0, 4, 2), (1, 0, 2), (1, 2, 4)):
                    o = (c * HC + h0) * P
                    mm = pe_.matmul(dst[:, o:o + n * P], qk[:, c, :], kb[:, c, h0:h0 + n, :].rearrange(
                        "p h n -> p (h n)"), start=True, stop=True)
                    if o == 0:
                        mm.then_inc(first_bank, 1)
                return mm

            def split(ap):
                return [ap[:, c * P:(c + 1) * P] for c in range(NC)]

            def a0_xT(t):
                pe_.wait_ge(x_ready, t + 1)
                if later(t):
                    pe_.wait_ge(pT_lo, t)
                if later(t):
                    pe_.wait_ge(pT_hi, t)
                transpose_pair(split(XT_A), x).then_inc(xT_ps, 1)

            def a1_qkv(t):
                pe_.wait_ge(xT_ready, t + 1)
                project(QK_A, wqkv_sb, xT).then_inc(qk_ps, 1)
                for k in range(NC):
                    mm = pe_.matmul(V_A, xT[:, k * P:(k + 1) * P], wqkv_sb[:, 2, k, :],
                                    start=(k == 0), stop=(k == NC - 1))
                mm.then_inc(v_ps, 1)

            def a2_scores(t):
                pe_.wait_ge(kbd_ready, NC * (t + 1))
                pe_.wait_ge(v_ready, t + 1)
                scores(SA, qkT, kbd, s_lo).then_inc(s_ps, 1)

            def a3_probT(t):
                pe_.wait_ge(pn_lo, t + 1)
                for h in range(H):
                    if h == 8:
                        pe_.wait_ge(pn_hi, t + 1)
                    mm = pe_.transpose(SA[:, h * P:(h + 1) * P], prob[:, h, :], id_sb[:])
                    if h == 3:
                        mm.then_inc(pT_bank0, 1)
                mm.then_inc(pT_ps, 1)

            def a4_o(t):
                pe_.wait_ge(pT_lo, t + 1)
                pe_.wait_ge(pT_hi, t + 1)
                if later(t - 1):
                    pe_.wait_ge(z_read, t - 1)
                for h in range(H):
                    c, j = divmod(h, HG)
                    mm = pe_.matmul(O_A[G * j:G * j + G, c * P:(c + 1) * P], vpad[:, h, :], probT[:, h, :],
                                    start=True, stop=True)
                mm.then_inc(o_ps, 1)

            def a5_y(t):
                pe_.wait_ge(o_ready, t + 1)
                if later(t):
                    pe_.wait_ge(h1T_ready, t)
                if later(t - 3):
                    pe_.wait_ge(x2nT_ready, t - 3)
                for c in range(NG):
                    mm = pe_.matmul(Y_A, oT[:, c * P:(c + 1) * P], wo_sb[:, c, :], start=(c == 0), stop=(c == NG - 1))
                mm.then_inc(y_ps, 1)

            def a6_h1T(t):
                pe_.wait_ge(h1_ready, t + 1)
                if later(t):
                    pe_.wait_ge(hid_b, t)
                transpose_pair(split(H1T_A), h1).then_inc(h1T_ps, 1)

            def a7_ff1(t):
                pe_.wait_ge(h1T_ready, t + 1)
                pe_.wait_ge(o_ready, upto(t + 2))
                pe_.wait_ge(y_read, upto(t + 2))
                if later(t):
                    pe_.wait_ge(z_read, t)
                if later(t - 2):
                    pe_.wait_ge(x2nT_ready, t - 2)
                for m in range(FM):
                    o = (m % 3) * P
                    dst = (N0 if m < 3 else N1)[:, o:o + P]
                    for k in range(NC):
                        mm = pe_.matmul(dst, w1_sb[:, k, m * P:(m + 1) * P], h1T[:, k * P:(k + 1) * P],
                                        start=(k == 0), stop=(k == NC - 1))
                    if m == 2:
                        mm.then_inc(fa_ps, 1)
                mm.then_inc(fb_ps, 1)

            def a8_ff2(t):
                pe_.wait_ge(hid_a, t + 1)
                pe_.wait_ge(hid_b, t + 1)
                if later(t - 2):
                    pe_.wait_ge(lgexp_ready, t - 2)
                for m in range(FM):
                    mm = pe_.matmul(Z_A, hid[:, m, :], w2_sb[:, m, :], start=(m == 0), stop=(m == FM - 1))
                mm.then_inc(z_ps, 1)

            def b0_xnT(t):
                pe_.wait_ge(xn_ready, t + 1)
                if later(t):
                    pe_.wait_ge(p2T_lo, t)
                    pe_.wait_ge(p2T_hi, t)
                transpose_pair(split(XNT_B), xn).then_inc(xnT_ps, 1)

            def b1_qk(t):
                pe_.wait_ge(xnT_ready, t + 1)
                project(QK_B, wa_sb, xnT).then_inc(qk2_ps, 1)

            def b2_tok(t):
                pe_.wait_ge(qk2_ready, t + 1)
                if later(t):
                    pe_.wait_ge(aT_ready, t)
                for n in range(2 * NC):
                    mm = pe_.transpose(TOK_B[:, n * C:(n + 1) * C], qk2T[:, n, :], id_sb[0:C, 0:C])
                mm.then_inc(tok_ps, 1)

            def b3_scores(t):
                pe_.wait_ge(kbd2_ready, t + 1)
                pe_.wait_ge(kbd2_hi, t + 1)
                pe_.wait_ge(tok_ready, t + 1)
                if later(t):
                    pe_.wait_ge(u_read, t)
                scores(SB, qk2T, kbd2, s2_lo).then_inc(s2_ps, 1)

            def b4_probT(t):
                pe_.wait_ge(pn2_lo, t + 1)
                for h in range(H):
                    if h == 8:
                        pe_.wait_ge(pn2_hi, t + 1)
                    mm = pe_.transpose(SB[:, h * P:(h + 1) * P], prob2[:, h, :], id_sb[:])
                    if h == 3:
                        mm.then_inc(p2T_bank0, 1)
                mm.then_inc(p2T_ps, 1)

            def b5_a(t):
                pe_.wait_ge(p2T_lo, t + 1)
                pe_.wait_ge(p2T_hi, t + 1)
                pe_.wait_ge(tok_ready, t + 1)
                for h in range(H):
                    c, j = divmod(h, HG)
                    dst = A_B[G * j:G * j + G, c * P:(c + 1) * P]
                    pe_.matmul(dst, kpad[:, h, :], prob2T[:, h, :], start=True, stop=False)
                    mm = pe_.matmul(dst, qpad[:, h, :], prob2[:, h, :], start=False, stop=True)
                mm.then_inc(a_ps, 1)

            def b6_u(t):
                pe_.wait_ge(aT_ready, t + 1)
                pe_.wait_ge(xnT_ready, upto(t + 2))
                for c in range(NG):
                    mm = pe_.matmul(U_B, aT[:, c * P:(c + 1) * P], wqk_sb[:, c, :], start=(c == 0), stop=(c == NG - 1))
                mm.then_inc(u_ps, 1)

            def b7_x2nT(t):
                pe_.wait_ge(x2n_ready, t + 1)
                pe_.wait_ge(h1T_ready, upto(t + 4))
                pe_.wait_ge(hid_b, upto(t + 3))
                transpose_pair(split(X2T_B), x2n).then_inc(x2nT_ps, 1)

            def b8_router(t):
                pe_.wait_ge(x2nT_ready, t + 1)
                pe_.wait_ge(hid_a, upto(t + 4))
                if later(t):
                    pe_.wait_ge(lgexp_ready, t)
                pe_.wait_ge(z_read, upto(t + 3))
                for k in range(NC):
                    mm = pe_.matmul(LG_B, x2nT[:, k * P:(k + 1) * P], rw_sb[:, k, :], start=(k == 0), stop=(k == NC - 1))
                mm.then_inc(lg_ps, 1)

            def body(i):
                at(i, 4, b3_scores)
                at(i, 1, a3_probT)
                at(i, 5, b7_x2nT)
                at(i, 0, a0_xT)
                at(i, 1, a4_o)
                at(i, 0, a1_qkv)
                at(i, 1, a5_y)
                at(i, 2, a7_ff1)
                at(i, 4, b4_probT)
                at(i, 1, a6_h1T)
                at(i, 5, b8_router)
                at(i, 0, a2_scores)
                at(i, 3, b0_xnT)
                at(i, 4, b5_a)
                at(i, 3, b1_qk)
                at(i, 4, b6_u)
                at(i, 3, b2_tok)
                at(i, 2, a8_ff2)

            tiles(pe_, body)

            pe_.wait_ge(imp_ready, 1)
            pe_.matmul(SA[:, 0:E], ones_sb[:], imp[:], start=True, stop=True).then_inc(imp_ps, 1)
            pe_.wait_ge(moe_in, 32)
            pe_.wait_ge(comb_ready, 1)

            def experts(i):
                steps = [(j, e) for j in range(2) for e in range(E)]

                def up(n):
                    j, e = steps[n]
                    s = 2 * E * i + n
                    if e == 0:
                        pe_.wait_ge(xe_in[j], 16 * (i + 1))
                    if later(s - 1):
                        pe_.wait_ge(eh_ready, s - 1)
                    for m in range(EM):
                        for k in range(NC):
                            o = e * EI + m * P
                            mm = pe_.matmul(ps[:, e % 2, m * P:(m + 1) * P], m1_sb[:, k, o:o + P],
                                            xe[:, j, k * P:(k + 1) * P], start=(k == 0), stop=(k == NC - 1))
                    mm.then_inc(w1_done, 1)

                def down(n):
                    e = steps[n][1]
                    s = 2 * E * i + n
                    pe_.wait_ge(eh_ready, s + 1)
                    if later(s - 1):
                        pe_.wait_ge(acc_step, s - 1)
                    for m in range(EM):
                        mm = pe_.matmul(ps[:, 2 + e % 2, 0:D], ehid[:, e % 2, m * P:(m + 1) * P], m2_sb[:, m, e, :],
                                        start=(m == 0), stop=(m == EM - 1))
                    mm.then_inc(w2_done, 1)

                up(0)
                for n in range(len(steps)):
                    if n + 1 < len(steps):
                        up(n + 1)
                    down(n)

            pairs(pe_, experts)

        @block.scalar
        def _(act):
            act.wait_ge(consts_in, 16 * len(CONSTS))

            def copy(dst, src):
                return act.activation(dst, src, ACT.Copy)

            def c_xT(t):
                act.wait_ge(xT_ps, t + 1)
                if later(t):
                    act.wait_ge(v_ps, t)
                copy(xT[:], XT_A).then_inc(xT_ready, 1)

            def exponentials(part, src, dst, nm, ls):
                for h in range(4 * part, 4 * part + 4):
                    a = act.activation(dst[:, h, :], src[:, h * P:(h + 1) * P], ACT.Exp, bias=nm[:, h:h + 1],
                                       accum_out=ls[:, h:h + 1])
                return a

            def c_exp(part):
                def stage(t):
                    if part == 0:
                        if later(t):
                            act.wait_ge(pT_ps, t)
                            act.wait_ge(r_ready, t)
                        act.wait_ge(nm_lo, t + 1)
                    if part == 1:
                        act.wait_ge(nm_ready, t + 1)
                    a = exponentials(part, SA, prob, nmax, lsum)
                    if part == 1:
                        a.then_inc(p_lo, 1)
                    if part == 2:
                        a.then_inc(p_ready, 1)
                return stage

            def c_exp2(part):
                def stage(t):
                    if part == 0:
                        if later(t):
                            act.wait_ge(a_ps, t)
                            act.wait_ge(r2_ready, t)
                        act.wait_ge(nm2_lo, t + 1)
                    if part == 1:
                        act.wait_ge(nm2_ready, t + 1)
                    a = exponentials(part, SB, prob2, nmax2, lsum2)
                    if part == 1:
                        a.then_inc(p2_lo, 1)
                    if part == 2:
                        a.then_inc(p2_ready, 1)
                return stage

            def c_pT(t):
                act.wait_ge(pT_bank0, t + 1)
                if later(t):
                    act.wait_ge(o_ps, t)
                copy(probT[:, 0:4, :].rearrange("p h n -> p (h n)"), SA[:, 0:512]).then_inc(pT_lo, 1)
                act.wait_ge(pT_ps, t + 1)
                copy(probT[:, 4:12, :].rearrange("p h n -> p (h n)"), SA[:, 512:1536]).then_inc(pT_hi, 1)

            def c_p2T(t):
                act.wait_ge(p2T_bank0, t + 1)
                if later(t):
                    act.wait_ge(a_ps, t)
                copy(prob2T[:, 0:4, :].rearrange("p h n -> p (h n)"), SB[:, 0:512]).then_inc(p2T_lo, 1)
                act.wait_ge(p2T_ps, t + 1)
                copy(prob2T[:, 4:12, :].rearrange("p h n -> p (h n)"), SB[:, 512:1536]).then_inc(p2T_hi, 1)

            def c_x2nT(t):
                act.wait_ge(x2nT_ps, t + 1)
                if later(t):
                    act.wait_ge(lg_ps, t)
                    act.wait_ge(stored, 16 * t)
                copy(x2nT[:], X2T_B).then_inc(x2nT_ready, 1)

            def c_o(t):
                act.wait_ge(o_ps, t + 1)
                if later(t):
                    act.wait_ge(y_ps, t)
                copy(oT[:], O_A).then_inc(o_ready, 1)

            def c_h1T(t):
                act.wait_ge(h1T_ps, t + 1)
                if later(t):
                    act.wait_ge(fb_ps, t)
                copy(h1T[:], H1T_A).then_inc(h1T_ready, 1)

            def c_hid(t):
                act.wait_ge(fa_ps, t + 1)
                if later(t):
                    act.wait_ge(z_ps, t)
                for m in range(FM):
                    if m == FM // 2:
                        act.wait_ge(fb_ps, t + 1)
                    src = (N0 if m < FM // 2 else N1)[:, (m % 3) * P:(m % 3 + 1) * P]
                    a = act.activation(hid[:, m, :], src, ACT.Relu, bias=b1_sb[:, m:m + 1])
                    if m == FM // 2 - 1:
                        a.then_inc(hid_a, 1)
                a.then_inc(hid_b, 1)

            def c_xnT(t):
                act.wait_ge(xnT_ps, t + 1)
                if later(t):
                    act.wait_ge(qk2_ps, t)
                copy(xnT[:], XNT_B).then_inc(xnT_ready, 1)

            def c_aT(t):
                act.wait_ge(a_ps, t + 1)
                if later(t):
                    act.wait_ge(u_ps, t)
                copy(aT[:], A_B).then_inc(aT_ready, 1)

            def c_lg(t):
                act.wait_ge(lgmax_ready, t + 1)
                if later(t):
                    act.wait_ge(probs_ready, t)
                act.activation(lg[:], LG_B, ACT.Exp, bias=lgmax[:], accum_out=lgsum[:]).then_inc(lgexp_ready, 1)

            def body(i):
                at(i, 1, c_pT)
                at(i, 5, c_x2nT)
                at(i, 0, c_xT)
                at(i, 4, c_exp2(0))
                at(i, 1, c_o)
                at(i, 4, c_exp2(1))
                at(i, 4, c_exp2(2))
                at(i, 2, c_hid)
                at(i, 4, c_p2T)
                at(i, 1, c_h1T)
                at(i, 5, c_lg)
                at(i, 3, c_xnT)
                at(i, 0, c_exp(0))
                at(i, 4, c_aT)
                at(i, 0, c_exp(1))
                at(i, 0, c_exp(2))

            tiles(act, body)

            def experts(i):
                for n in range(2 * E):
                    s = 2 * E * i + n
                    act.wait_ge(w1_done, s + 1)
                    if later(s - 1):
                        act.wait_ge(w2_done, s - 1)
                    act.activation(ehid[:, n % 2, :], ps[:, n % 2, :], ACT.Silu).then_inc(eh_ready, 1)

            pairs(act, experts)

        @block.vector
        def _(dve):
            dve.wait_ge(tok_in, 16)
            dve.tensor_scalar(neg_sb[:], tok_sb[:], 0.0, float(V), ALU.is_lt, ALU.mult).then_inc(tok_step, 1)
            dve.wait_ge(tok_step, 1)
            dve.tensor_tensor(tok_sb[:], tok_sb[:], neg_sb[:], ALU.add).then_inc(tok_step, 1)
            dve.wait_ge(tok_step, 2)
            dve.tensor_scalar(tok_sb[:], tok_sb[:], 0.0, float(V - 1), ALU.max, ALU.min).then_inc(tok_fixed, 1)
            dve.wait_ge(consts_in, 16 * len(CONSTS))
            dve.wait_ge(setup, 8)
            dve.tensor_scalar(maska_sb[:], mask_sb[:], float(HD) ** -0.5, None, ALU.mult).then_inc(mask_step, 1)
            for c in range(NC):
                dve.tensor_scalar(maskb_sb[:, c, :], mask_sb[:], betas_sb[:, c:c + 1], None,
                                  ALU.mult).then_inc(mask_step, 1)
            dve.tensor_copy(iotaf_sb[:], iota_sb[:]).then_inc(mask_step, 1)
            dve.wait_ge(mask_step, 4)

            ticks = [0]

            def tick():
                k = ticks[0] = (ticks[0] + 1) % 16
                dve.memset(tick_sb[:, k:k + 1], 0.0)

            def v_qk(t):
                dve.wait_ge(qk_ps, t + 1)
                if later(t):
                    dve.wait_ge(s_ps, t)
                dve.tensor_tensor(qkT[:], QK_A.rearrange("p (n k) -> p n k", n=2 * NC),
                                  bqk_sb[:, :, None].broadcast_to([C, 2 * NC, P]), ALU.add).then_inc(qk_ready, 1)
                dve.wait_ge(v_ps, t + 1)
                if later(t):
                    dve.wait_ge(o_ps, t)
                dve.tensor_tensor(vpad[:, :, 0:HD], V_A.rearrange("p (h d) -> p h d", h=H),
                                  row["bv"].rearrange("p (h d) -> p h d", h=H), ALU.add).then_inc(v_ready, 1)

            def v_max(t):
                if later(t):
                    dve.wait_ge(p_ready, t)
                dve.wait_ge(s_lo, t + 1)
                dve.tensor_reduce(nmax[:, 0:4], SA[:, 0:512].rearrange("p (h n) -> p h n", h=4), AX.X, ALU.max,
                                  negate=True).then_inc(nm_lo, 1)
                dve.wait_ge(s_ps, t + 1)
                dve.tensor_reduce(nmax[:, 4:12], SA[:, 512:1536].rearrange("p (h n) -> p h n", h=8), AX.X, ALU.max,
                                  negate=True).then_inc(nm_ready, 1)

            def v_max2(t):
                if later(t):
                    dve.wait_ge(p2_ready, t)
                dve.wait_ge(s2_lo, t + 1)
                dve.tensor_reduce(nmax2[:, 0:4], SB[:, 0:512].rearrange("p (h n) -> p h n", h=4), AX.X, ALU.max,
                                  negate=True).then_inc(nm2_lo, 1)
                dve.wait_ge(s2_ps, t + 1)
                dve.tensor_reduce(nmax2[:, 4:12], SB[:, 512:1536].rearrange("p (h n) -> p h n", h=8), AX.X, ALU.max,
                                  negate=True).then_inc(nm2_ready, 1)

            def v_norm(t):
                if later(t):
                    dve.wait_ge(pn_lo, t)
                    dve.wait_ge(pn_hi, t)
                dve.wait_ge(p_lo, t + 1)
                dve.reciprocal(rsum[:, 0:8], lsum[:, 0:8]).then_inc(r_lo, 1)
                dve.wait_ge(r_lo, t + 1)
                dve.tensor_tensor(prob[:, 0:8, :], prob[:, 0:8, :], rsum[:, 0:8, None].broadcast_to([P, 8, P]),
                                  ALU.mult).then_inc(pn_lo, 1)
                dve.wait_ge(p_ready, t + 1)
                dve.reciprocal(rsum[:, 8:12], lsum[:, 8:12]).then_inc(r_ready, 1)

            def v_norm2(t):
                if later(t):
                    dve.wait_ge(pn2_lo, t)
                    dve.wait_ge(pn2_hi, t)
                dve.wait_ge(p2_lo, t + 1)
                dve.reciprocal(rsum2[:, 0:8], lsum2[:, 0:8]).then_inc(r2_lo, 1)
                dve.wait_ge(r2_lo, t + 1)
                dve.tensor_tensor(prob2[:, 0:8, :], prob2[:, 0:8, :], rsum2[:, 0:8, None].broadcast_to([P, 8, P]),
                                  ALU.mult).then_inc(pn2_lo, 1)
                dve.wait_ge(p2_ready, t + 1)
                dve.reciprocal(rsum2[:, 8:12], lsum2[:, 8:12]).then_inc(r2_ready, 1)

            def stats(n, t, src):
                tick()
                dve.bn_stats(st[n][:], src).then_inc(st_ready[n], 1)
                yield
                dve.wait_ge(st_ready[n], t + 1)
                tick()
                dve.bn_aggr(mv[n][:], st[n][:]).then_inc(mv_ready[n], 1)
                yield
                dve.wait_ge(mv_ready[n], t + 1)

            def tok_norm(n, t, src, tmp, gamma):
                dve.scalar_tensor_tensor(tmp, src, mv[n][:, 0:1], gamma, ALU.subtract, ALU.mult).then_inc(shifted[n], 1)
                yield
                dve.wait_ge(std_ready[n], t + 1)
                dve.tensor_scalar(sd[n][:], sd[n][:], EPS_TOK, None, ALU.add).then_inc(sd_ready[n], 1)
                yield
                dve.wait_ge(sd_ready[n], t + 1)
                dve.reciprocal(rstd[n][:], sd[n][:]).then_inc(rstd_ready[n], 1)
                yield
                dve.wait_ge(rstd_ready[n], t + 1)
                dve.wait_ge(shifted[n], t + 1)

            def v_y(t):
                dve.wait_ge(y_ps, t + 1)
                dve.wait_ge(res_ready, t + 1)
                dve.tensor_tensor(y[:], Y_A, hrow(t), ALU.add).then_inc(y_read, 1)
                yield
                dve.wait_ge(y_read, t + 1)
                yield from stats(0, t, y[:])
                yield from tok_norm(0, t, y[:], yc[:], row["gamma1"])
                if later(t):
                    dve.wait_ge(h1T_ps, t)
                    dve.wait_ge(h1b_ready, t)
                dve.scalar_tensor_tensor(h1[:], yc[:], rstd[0][:], row["beta1"], ALU.mult,
                                         ALU.add).then_inc(h1_ready, 1)

            def v_zread(t):
                dve.wait_ge(z_ps, t + 1)
                dve.wait_ge(h1b_ready, t + 1)
                dve.tensor_tensor(z[:], Z_A, hrow(t), ALU.add).then_inc(z_read, 1)

            def v_z(t):
                dve.wait_ge(z_read, t + 1)
                yield from stats(1, t, z[:])
                yield from tok_norm(1, t, z[:], zc[:], row["gamma2"])
                dve.scalar_tensor_tensor(hs[:], zc[:], rstd[1][:], row["beta2"], ALU.mult,
                                         ALU.add).then_inc(hs_ready, 1)
                yield
                dve.wait_ge(hs_ready, t + 1)
                yield from stats(2, t, hs[:])
                tick()
                dve.tensor_copy(hrow(t), hs[:]).then_inc(h_ready, 1)

            def v_xn(t):
                dve.wait_ge(std_ready[2], t + 1)
                if later(t):
                    dve.wait_ge(xnT_ps, t)
                dve.tensor_scalar(xn[:], hs[:], mv[2][:, 0:1], rstd[2][:], ALU.subtract,
                                  ALU.mult).then_inc(xn_ready, 1)

            def v_u(t):
                dve.wait_ge(u_ps, t + 1)
                dve.wait_ge(h_ready, t + 1)
                dve.tensor_tensor(h2[:], U_B, hrow(t), ALU.add).then_inc(u_read, 1)
                yield
                dve.wait_ge(u_read, t + 1)
                yield from stats(3, t, h2[:])
                tick()
                dve.tensor_copy(hrow(t), h2[:])

            def v_x2n(t):
                dve.wait_ge(std_ready[3], t + 1)
                if later(t):
                    dve.wait_ge(x2nT_ps, t)
                dve.tensor_scalar(x2n[:], h2[:], mv[3][:, 0:1], rstd[3][:], ALU.subtract,
                                  ALU.mult).then_inc(x2n_ready, 1)

            def in_turns(*stages):
                stages = list(stages)
                while stages:
                    stages = [g for g in stages if next(g, stages) is not stages]

            def v_tok(t):
                dve.wait_ge(tok_ps, t + 1)
                if later(t):
                    dve.wait_ge(a_ps, t)
                dve.tensor_copy(qpad[:, :, HD:G], TOK_B[:, 0:D].rearrange("p (h d) -> p h d", h=H))
                dve.tensor_copy(kpad[:, :, 0:HD], TOK_B[:, D:2 * D].rearrange("p (h d) -> p h d", h=H)
                                ).then_inc(tok_ready, 1)

            def v_qk2(t):
                dve.wait_ge(qk2_ps, t + 1)
                if later(t):
                    dve.wait_ge(s2_ps, t)
                dve.tensor_copy(qk2T[:].rearrange("p n k -> p (n k)"), QK_B).then_inc(qk2_ready, 1)

            def v_spread_k2(t):
                dve.wait_ge(qk2_ready, t + 1)
                dve.tensor_tensor(kbd2[:, 1, :, :], qk2T[:, NC + 1:NC + 2, :].broadcast_to([C, HC, P]),
                                  maskb_sb[:, 1, :, None].broadcast_to([C, HC, P]), ALU.mult).then_inc(kbd2_hi, 1)

            def v_lgmax(t):
                dve.wait_ge(lg_ps, t + 1)
                dve.tensor_reduce(lgmax[:], LG_B, AX.X, ALU.max, negate=True).then_inc(lgmax_ready, 1)

            def v_probs(t):
                dve.wait_ge(lgexp_ready, t + 1)
                dve.reciprocal(lginv[:], lgsum[:]).then_inc(lginv_ready, 1)
                yield
                dve.wait_ge(lginv_ready, t + 1)
                dve.tensor_scalar(pr[:], lg[:], lginv[:], None, ALU.mult).then_inc(pr_ready, 1)
                yield
                dve.wait_ge(pr_ready, t + 1)
                tick()
                dve.tensor_copy(probs_all[:, bass.ds(t, 1), :].rearrange("p a e -> p (a e)"), pr[:])
                dve.max(top8[:], pr[:]).then_inc(top8_ready, 1)
                yield
                dve.wait_ge(top8_ready, t + 1)
                tick()
                dve.max_index(idx8[:], top8[:], pr[:]).then_inc(idx8_ready, 1)
                yield
                dve.wait_ge(idx8_ready, t + 1)
                tick()
                dve.tensor_copy(idx_all[:, bass.ds(t, 1), :].rearrange("p a e -> p (a e)"),
                                idx8[:, 0:2]).then_inc(probs_ready, 1)

            def tile_stage(i, skew, stage):
                if isinstance(i, int) and not 0 <= i - skew < T:
                    return iter(())
                return stage(i - skew)

            def body(i):
                at(i, 3, v_zread)
                at(i, 4, v_max2)
                at(i, 0, v_qk)
                in_turns(tile_stage(i, 1, v_y), tile_stage(i, 3, v_z))
                at(i, 4, v_norm2)
                at(i, 3, v_xn)
                at(i, 5, v_lgmax)
                at(i, 0, v_max)
                at(i, 3, v_qk2)
                at(i, 3, v_spread_k2)
                in_turns(tile_stage(i, 4, v_u), tile_stage(i, 5, v_probs))
                at(i, 3, v_tok)
                at(i, 4, v_x2n)
                at(i, 0, v_norm)

            tiles(dve, body)

            dve.wait_ge(probs_ready, T)
            dve.tensor_reduce(imp[:], probs_all[:].rearrange("p t e -> p e t"), AX.X, ALU.add).then_inc(imp_ready, 1)
            dve.tensor_copy(idxf[:], idx_all[:]).then_inc(comb_step, 1)
            dve.wait_ge(comb_step, 1)
            iota_b = iotaf_sb[:, None, :].broadcast_to([P, T, E])
            dve.tensor_tensor(one1[:], idxf[:, :, 0:1].broadcast_to([P, T, E]), iota_b, ALU.is_equal).then_inc(comb_step, 1)
            dve.wait_ge(comb_step, 2)
            dve.tensor_tensor(one2[:], idxf[:, :, 1:2].broadcast_to([P, T, E]), iota_b, ALU.is_equal).then_inc(comb_step, 1)
            dve.wait_ge(comb_step, 3)
            dve.tensor_tensor(one1[:], one1[:], one2[:], ALU.add).then_inc(comb_step, 1)
            dve.wait_ge(comb_step, 4)
            dve.wait_ge(imp_ps, 1)
            dve.tensor_scalar(rinv[:], SA[:, 0:E], -1.0, 1.0 - 0.9, ALU.add, ALU.mult).then_inc(comb_step, 1)
            dve.wait_ge(comb_step, 5)
            dve.tensor_scalar(rinv[:], rinv[:], 1.0, 0.01, ALU.add, ALU.add).then_inc(comb_step, 1)
            dve.wait_ge(comb_step, 6)
            dve.reciprocal(rinv[:], rinv[:]).then_inc(comb_step, 1)
            dve.wait_ge(comb_step, 7)
            dve.tensor_tensor(comb[:], probs_all[:], rinv[:, None, :].broadcast_to([P, T, E]), ALU.mult).then_inc(comb_step, 1)
            dve.wait_ge(comb_step, 8)
            dve.tensor_tensor(comb[:], comb[:], one1[:], ALU.mult).then_inc(comb_step, 1)
            dve.wait_ge(comb_step, 9)
            dve.tensor_reduce(csum[:], comb[:], AX.X, ALU.add).then_inc(comb_step, 1)
            dve.wait_ge(comb_step, 10)
            dve.reciprocal(csum[:], csum[:]).then_inc(comb_step, 1)
            dve.wait_ge(comb_step, 11)
            dve.tensor_tensor(comb[:], comb[:], csum[:, :, None].broadcast_to([P, T, E]),
                              ALU.mult).then_inc(comb_ready, 1)
            dve.wait_ge(comb_ready, 1)
            def experts(i):
                for j in range(2):
                    t = 2 * i + j
                    for e in range(E):
                        s = t * E + e
                        dve.wait_ge(w2_done, s + 1)
                        if later(s):
                            dve.wait_ge(acc_step, s)
                        cw = comb[:, bass.ds(t, 1), e:e + 1].rearrange("p a n -> p (a n)")
                        dve.scalar_tensor_tensor(hrow(t), ps[:, 2 + e % 2, 0:D], cw, hrow(t), ALU.mult,
                                                 ALU.add).then_inc(acc_step, 1)

            pairs(dve, experts)


def position_table():
    import numpy as np
    pos = np.arange(P, dtype=np.float32)[:, None]
    i = np.arange(D, dtype=np.float32)[None, :]
    ang = pos / np.power(np.float32(10000.0), np.float32(2.0) * i / np.float32(D))
    return np.where((np.arange(D) % 2 == 0)[None, :], np.cos(ang), np.sin(ang)).astype(np.float32)


def lay_out(a):
    import numpy as np

    def chunks(w, rows):
        return w.reshape(w.shape[0] // rows, rows, -1).transpose(1, 0, 2)

    def heads(first, second):
        w = np.zeros((H, 2, HD, D), np.float32)
        w[:, 0] = first.reshape(H, HD, D)
        if second is not None:
            w[:, 1] = second.reshape(H, HD, D)
        return chunks(w.reshape(H * G, D), P)

    row_names = [a["L0_tok_" + n] for n in ROWS]
    return {
        "tok": a["x"].T,
        "emb": a["L0_tok_emb"],
        "pe": position_table(),
        "ident": np.eye(P, dtype=np.float32),
        "hmask": (np.arange(C)[:, None] // HD == np.arange(HC)[None, :]).astype(np.float32),
        "w_qkv": np.stack([chunks(a["L0_tok_" + n], C) for n in ("wq", "wk", "wv")], 1),
        "bqk": np.concatenate([a["L0_tok_bq"].reshape(NC, C), a["L0_tok_bk"].reshape(NC, C)]).T,
        "rows": np.broadcast_to(np.stack(row_names)[None], (P, len(ROWS), D)),
        "wo": heads(a["L0_tok_wo"], None),
        "w1": chunks(a["L0_tok_w1"], C),
        "b1": a["L0_tok_b1"].reshape(FM, P).T,
        "w2": chunks(a["L0_tok_w2"], P),
        "wa": np.stack([chunks(a["L0_attn_Wq"].T, C), chunks(a["L0_attn_Wk"].T, C)], 1),
        "betas": np.repeat(a["L0_attn_betas"], HD).reshape(NC, C).T,
        "wqk": heads(a["L0_attn_Wq"], a["L0_attn_Wk"]),
        "rw": chunks(a["L0_ffn_router_w"].T, C),
        "m1": chunks(a["L0_ffn_w1"].transpose(2, 0, 1).reshape(D, E * EI), C),
        "m2": a["L0_ffn_w2"].transpose(2, 0, 1).reshape(EM, P, E, D).transpose(1, 0, 2, 3),
    }


def kernel(**inputs):
    import numpy as np
    import concourse.bacc as bacc
    from concourse.bass_utils import run_bass_kernel_spmd

    nc = bacc.Bacc("TRN2", target_bir_lowering=False, num_devices=1)
    arrays, args = {}, {}
    for name, a in lay_out({k: np.asarray(v) for k, v in inputs.items()}).items():
        arrays[f"in_{name}"] = np.ascontiguousarray(a)
        args[name] = nc.dram_tensor(f"in_{name}", a.shape, mybir.dt.from_np(a.dtype), kind="ExternalInput").ap()
    out = nc.dram_tensor("out", (T, P, D), F32, kind="ExternalOutput").ap()
    scratch = nc.dram_tensor("scratch", (T, C, NC * P), F32, kind="Internal").ap()
    tower_kernel(nc, out=out, scratch=scratch, **args)
    r = run_bass_kernel_spmd(nc, [arrays], core_ids=[0])
    return r.results[0]["out"]
```

```python
from contextlib import ExitStack

import concourse.bass as bass
from concourse import mybir

ALU = mybir.AluOpType
ACT = mybir.ActivationFunctionType
AX = mybir.AxisListType
F32 = mybir.dt.float32
I32 = mybir.dt.int32
U32 = mybir.dt.uint32
BF16 = mybir.dt.bfloat16

P = 128
T = 64
D = 192
C = 96
NC = D // C
H = 12
HD = D // H
HC = C // HD
G = 32
HG = P // G
NG = H // HG
FF = 768
FM = FF // P
V = 8000
E = 8
EI = 512
EM = EI // P
EPS_TOK = 1e-05
EPS_LN = 1e-05
K = 2
R = T * P + P
SLOTS = 4 * -(-(K * T + E) // 4)
SPARE = SLOTS - K * T
PICKED = K * T * P
W = D + 1
U = 4
CT = 4
ROWS = ("bv", "bo", "b2", "gamma1", "beta1", "gamma2", "beta2")
SKEW = 6


def tower_kernel(nc, tok, emb, pe, ident, hmask, w_qkv, bqk, rows, wo, w1, b1, w2, wa, betas, wqk,
                 rw, m1, m2, tri, counts, tile_no, out, regions, picked):
    ctx = ExitStack()
    with ctx:
        def sb(name, shape, dt=F32):
            return ctx.enter_context(nc.sbuf_tensor(name, shape, dt))

        def sem(name):
            return ctx.enter_context(nc.semaphore(name))

        tok_sb = sb("tok_sb", [P, T], I32)
        neg_sb = sb("neg_sb", [P, T], I32)
        pe_sb = sb("pe_sb", [P, D])
        id_sb = sb("id_sb", [P, P])
        mask_sb = sb("mask_sb", [C, HC])
        maska_sb = sb("maska_sb", [C, HC])
        maskb_sb = sb("maskb_sb", [C, NC, HC])
        betas_sb = sb("betas_sb", [C, NC])
        wqkv_sb = sb("wqkv_sb", [C, 3, NC, D])
        bqk_sb = sb("bqk_sb", [C, 2 * NC])
        rows_sb = sb("rows_sb", [P, len(ROWS), D])
        wo_sb = sb("wo_sb", [P, NG, D])
        w1_sb = sb("w1_sb", [C, NC, FF])
        b1_sb = sb("b1_sb", [P, FM])
        w2_sb = sb("w2_sb", [P, FM, D])
        wa_sb = sb("wa_sb", [C, 2, NC, D])
        wqk_sb = sb("wqk_sb", [P, NG, D])
        rw_sb = sb("rw_sb", [C, NC, E])
        m1_sb = sb("m1_sb", [C, NC, E * EI])
        m2_sb = sb("m2_sb", [P, EM, E, D])
        half_sb = sb("half_sb", [P, 1])
        mhalf_sb = sb("mhalf_sb", [P, 1])
        eps_sb = sb("eps_sb", [P, 1])
        tick_sb = sb("tick_sb", [P, 16])
        ptick_sb = sb("ptick_sb", [P, 2 + U])
        ones_sb = sb("ones_sb", [P, P])
        tile_rows_sb = sb("tile_rows_sb", [P, K])
        tri_bf = sb("tri_bf", [P, P], BF16)
        ones_bf = sb("ones_bf", [P, P], BF16)
        counts_sb = sb("counts_sb", [P, 2 * E + K + 2 * SPARE])
        expert_no = counts_sb[:, 0:E]
        region_no = counts_sb[:, E:2 * E]
        picked_no = counts_sb[:, 2 * E:2 * E + K]
        zero_no = counts_sb[:, 2 * E + K:2 * E + K + SPARE]
        spare_no = counts_sb[:, 2 * E + K + SPARE:2 * E + K + 2 * SPARE]
        tile_no_sb = sb("tile_no_sb", [1, SLOTS])
        row = {name: rows_sb[:, i, :] for i, name in enumerate(ROWS)}

        h_all = sb("h_all", [P, T, D])
        probs_all = sb("probs_all", [P, T, E])
        route_all = sb("route_all", [P, T, 2 * K])

        idx_now = sb("idx_now", [P, 1], U32)
        xg = sb("xg", [P, D])
        x = sb("x", [P, D])
        xT = sb("xT", [C, NC * P])
        qkT = sb("qkT", [C, 2 * NC, P])
        kbd = sb("kbd", [C, NC, HC, P])
        vpad = sb("vpad", [P, H, G])
        prob = sb("prob", [P, H, P])
        probT = sb("probT", [P, H, P])
        nmax = sb("nmax", [P, H])
        lsum = sb("lsum", [P, H])
        rsum = sb("rsum", [P, H])
        oT = sb("oT", [P, NG * P])
        y = sb("y", [P, D])
        h1 = sb("h1", [P, D])
        h1T = sb("h1T", [C, NC * P])
        hid = sb("hid", [P, FM, P])
        z = sb("z", [P, D])
        yc = sb("yc", [P, D])
        zc = sb("zc", [P, D])
        hs = sb("hs", [P, D])
        h2 = sb("h2", [P, D])
        xn = sb("xn", [P, D])
        xnT = sb("xnT", [C, NC * P])
        qk2T = sb("qk2T", [C, 2 * NC, P])
        kbd2 = sb("kbd2", [C, NC, HC, P])
        kpad = sb("kpad", [P, H, G])
        qpad = sb("qpad", [P, H, G])
        prob2 = sb("prob2", [P, H, P])
        zero_rows = sb("zero_rows", [P, SPARE, W])
        prob2T = zero_rows[:].rearrange("p s w -> p (s w)")[:, 0:H * P].rearrange("p (h n) -> p h n", h=H)
        nmax2 = sb("nmax2", [P, H])
        lsum2 = sb("lsum2", [P, H])
        rsum2 = sb("rsum2", [P, H])
        aT = sb("aT", [P, NG * P])
        x2n = sb("x2n", [P, D])
        x2nT = sb("x2nT", [C, NC * P])
        lg = sb("lg", [P, 8])
        lgmax = sb("lgmax", [P, 1])
        lgsum = sb("lgsum", [P, 1])
        lginv = sb("lginv", [P, 1])
        pr = sb("pr", [P, E])
        top8 = sb("top8", [P, 8])
        idx8 = sb("idx8", [P, 8], U32)
        route = sb("route", [P, 2 * K])
        chosen = sb("chosen", [P, K, E])
        chosen_sum = sb("chosen_sum", [P, E], BF16)
        filled = sb("filled", [P, E])
        place = sb("place", [P, E])
        placed = sb("placed", [P, K, E])
        slotf = sb("slotf", [P, K])
        slot = [sb(f"slot{k}", [P, 1], U32) for k in range(K)]
        xs = sb("xs", [P, K, W])
        st = [sb(f"st{i}", [P, 6]) for i in range(4)]
        mv = [sb(f"mv{i}", [P, 2]) for i in range(4)]
        sd = [sb(f"sd{i}", [P, 1]) for i in range(4)]
        rstd = [sb(f"rstd{i}", [P, 1]) for i in range(4)]

        imp = sb("imp", [P, E])
        rinv = sb("rinv", [P, E])
        until = [sb(f"until{n}", [P, 2 * E]) for n in range(4)]
        step_of = sb("step_of", [P, E])
        filled_tab = sb("filled_tab", [1, E], I32)
        before = prob[0:1, :, :].rearrange("p h n -> p (h n)")[:, 0:SLOTS * E].rearrange("p (s e) -> p s e", e=E)
        steps = probT[0:1, :, :].rearrange("p h n -> p (h n)")[:, 0:SLOTS * E].rearrange("p (s e) -> p s e", e=E)
        expert_f = qkT[0:1, 0:2, :].rearrange("p n k -> p (n k)")[:, 0:SLOTS]
        first_f = qkT[0:1, 2:4, :].rearrange("p n k -> p (n k)")[:, 0:SLOTS]
        expert_tab = sb("expert_tab", [1, SLOTS], I32)
        first_tab = sb("first_tab", [1, SLOTS], I32)
        bal = hid[:, 0:4, :].rearrange("p m n -> p (m n)").rearrange("p (t e) -> p t e", e=E)
        share = sb("share", [P, T, K])
        csum = sb("csum", [P, T])
        dest = [sb(f"dest{b}", [P, 1], U32) for b in range(U)]
        xr = probT[:].rearrange("p h n -> p (h n)")[:, 0:U * W].rearrange("p (b w) -> p b w", b=U)
        xeT = kbd[:, 0, 0:4, :].rearrange("p (s c) n -> p s (c n)", s=2)
        ehid = prob[:, 0:8, :].rearrange("p (s m) n -> p s (m n)", s=2)
        ehT = prob2[:, 0:8, :].rearrange("p (s m) n -> p s (m n)", s=2)
        yo = prob[:, 8:11, :].rearrange("p h n -> p (h n)").rearrange("p (s d) -> p s d", s=2)
        yk = [buf.rearrange("p h n -> p (h n)").rearrange("p (k t d) -> p k t d", k=K, t=CT)
              for buf in (prob2[:], prob2T, prob[:], probT[:])]
        YB = len(yk)

        ps = ctx.enter_context(nc.psum_tensor("ps", [P, 8, 512], F32))
        flat = ps[:, :, :].rearrange("p b n -> p (b n)")
        SA = flat[:, 0:1536]
        SB = flat[:, 1536:3072]
        N0 = flat[:, 3072:3584]
        N1 = flat[:, 3584:4096]
        QK_A = SA[0:C, 1024:1536]
        V_A = SA[:, 512:704]
        XT_A = SA[0:C, 0:256]
        O_A = N0[:, 0:384]
        Y_A = N1[:, 0:192]
        H1T_A = N1[0:C, 192:448]
        Z_A = N0[:, 0:192]
        XNT_B = SB[0:C, 1280:1536]
        QK_B = SB[0:C, 0:512]
        TOK_B = SB[:, 512:896]
        A_B = SB[:, 512:896]
        U_B = SB[:, 1024:1216]
        X2T_B = N1[0:C, 0:256]
        LG_B = N0[:, 256:264]
        RANK_B = SA[:, 768:768 + E]
        COUNT_B = SA[:, 768 + E:768 + 2 * E]
        IMP = SA[:, 0:E]

        tok_in = sem("tok_in")
        consts_in = sem("consts_in")
        late_in = sem("late_in")
        moe_in = sem("moe_in")
        setup = sem("setup")
        tok_step = sem("tok_step")
        tok_fixed = sem("tok_fixed")
        mask_step = sem("mask_step")
        idx_ready = sem("idx_ready")
        rows_in = sem("rows_in")
        x_ready = sem("x_ready")
        res_ready = sem("res_ready")
        xT_ps = sem("xT_ps")
        xT_ready = sem("xT_ready")
        qk_ps = sem("qk_ps")
        v_ps = sem("v_ps")
        qk_ready = sem("qk_ready")
        v_ready = sem("v_ready")
        kbd_ready = sem("kbd_ready")
        kbd_hi = sem("kbd_hi")
        s_lo = sem("s_lo")
        s_ps = sem("s_ps")
        nm_lo = sem("nm_lo")
        p_lo = sem("p_lo")
        r_lo = sem("r_lo")
        nm_ready = sem("nm_ready")
        p_ready = sem("p_ready")
        r_ready = sem("r_ready")
        pn_lo = sem("pn_lo")
        pn_hi = sem("pn_hi")
        pT_bank0 = sem("pT_bank0")
        pT_bank1 = sem("pT_bank1")
        pT_ps = sem("pT_ps")
        pT_lo = sem("pT_lo")
        pT_mid = sem("pT_mid")
        pT_hi = sem("pT_hi")
        o_ps = sem("o_ps")
        o_ready = sem("o_ready")
        y_ps = sem("y_ps")
        y_read = sem("y_read")
        h1_ready = sem("h1_ready")
        h1T_ps = sem("h1T_ps")
        h1T_ready = sem("h1T_ready")
        fa_ps = sem("fa_ps")
        fb_ps = sem("fb_ps")
        hid_ready = sem("hid_ready")
        z_ps = sem("z_ps")
        z_read = sem("z_read")
        hs_ready = sem("hs_ready")
        h_ready = sem("h_ready")
        h1b_ready = sem("h1b_ready")
        xn_ready = sem("xn_ready")
        xnT_ps = sem("xnT_ps")
        xnT_ready = sem("xnT_ready")
        qk2_ps = sem("qk2_ps")
        qk2_ready = sem("qk2_ready")
        kbd2_ready = sem("kbd2_ready")
        kbd2_hi = sem("kbd2_hi")
        tok_ps = sem("tok_ps")
        tok_ready = sem("tok_ready")
        s2_lo = sem("s2_lo")
        s2_ps = sem("s2_ps")
        nm2_lo = sem("nm2_lo")
        p2_lo = sem("p2_lo")
        r2_lo = sem("r2_lo")
        nm2_ready = sem("nm2_ready")
        p2_ready = sem("p2_ready")
        r2_ready = sem("r2_ready")
        pn2_lo = sem("pn2_lo")
        pn2_hi = sem("pn2_hi")
        p2T_bank0 = sem("p2T_bank0")
        p2T_bank1 = sem("p2T_bank1")
        p2T_ps = sem("p2T_ps")
        p2T_hi = sem("p2T_hi")
        a_ps = sem("a_ps")
        aT_ready = sem("aT_ready")
        u_ps = sem("u_ps")
        u_read = sem("u_read")
        x2n_ready = sem("x2n_ready")
        x2nT_ps = sem("x2nT_ps")
        x2nT_ready = sem("x2nT_ready")
        lg_ps = sem("lg_ps")
        lgmax_ready = sem("lgmax_ready")
        lgexp_ready = sem("lgexp_ready")
        lginv_ready = sem("lginv_ready")
        pr_ready = sem("pr_ready")
        top8_ready = sem("top8_ready")
        idx8_ready = sem("idx8_ready")
        route_ready = sem("route_ready")
        chosen_ready = sem("chosen_ready")
        sum_ready = sem("sum_ready")
        rank_ps = sem("rank_ps")
        place_ready = sem("place_ready")
        filled_ready = sem("filled_ready")
        placed_ready = sem("placed_ready")
        slotf_ready = sem("slotf_ready")
        slot_ready = sem("slot_ready")
        xs_ready = sem("xs_ready")
        ids_ready = sem("ids_ready")
        scattered = sem("scattered")
        zeros_ready = sem("zeros_ready")
        filled_out = sem("filled_out")
        spare_out = sem("spare_out")
        zeros_out = sem("zeros_out")
        imp_ready = sem("imp_ready")
        imp_ps = sem("imp_ps")
        imp_read = sem("imp_read")
        table_step = sem("table_step")
        table_ready = sem("table_ready")
        share_step = sem("share_step")
        xr_in = [sem(f"xr_in{b}") for b in range(U)]
        y_out = [sem(f"y_out{b}") for b in range(U)]
        xe_ps = sem("xe_ps")
        xe_ready = sem("xe_ready")
        dest_ready = sem("dest_ready")
        up_ps = sem("up_ps")
        eh_ready = sem("eh_ready")
        ehT_ps = sem("ehT_ps")
        ehT_ready = sem("ehT_ready")
        down_ps = sem("down_ps")
        yo_ready = sem("yo_ready")
        carried = sem("carried")
        yk_in = [sem(f"yk_in{b}") for b in range(4)]
        first_added = sem("first_added")
        both_added = sem("both_added")
        out_done = sem("out_done")
        st_ready = [sem(f"st_ready{n}") for n in range(4)]
        mv_ready = [sem(f"mv_ready{n}") for n in range(4)]
        shifted = [sem(f"shifted{n}") for n in range(2)]
        var_ready = [sem(f"var_ready{n}") for n in range(4)]
        std_ready = [sem(f"std_ready{n}") for n in range(4)]
        sd_ready = [sem(f"sd_ready{n}") for n in range(2)]
        rstd_ready = [sem(f"rstd_ready{n}") for n in range(2)]

        def later(n):
            return not isinstance(n, int) or n > 0

        def tiles(eng, body):
            for i in range(SKEW + 1):
                body(i)
            with eng.Fori(SKEW + 1, T - 1) as i:
                body(i)
            for i in range(T - 1, T + SKEW):
                body(i)

        def peeled(t):
            return isinstance(t, int)

        def upto(n):
            return min(n, T) if isinstance(n, int) else n

        def slot_tiles(eng, body):
            for n in range(U):
                body(0, n)
            with eng.Fori(1, SLOTS // U - 1) as g:
                for n in range(U):
                    body(g, n)
            for n in range(U):
                body(SLOTS // U - 1, n)

        def sum_steps(eng, body):
            for b in range(YB):
                body(0, b)
            with eng.Fori(1, T // CT // YB) as i:
                for b in range(YB):
                    body(i, b)

        def at(i, skew, stage):
            t = i - skew
            if isinstance(i, int) and not 0 <= t < T:
                return
            stage(t)

        def hrow(t):
            return h_all[:, bass.ds(t, 1), :].rearrange("p a n -> p (a n)")

        block = ctx.enter_context(nc.Block())

        CONSTS = [(id_sb[:], ident), (mask_sb[:], hmask), (betas_sb[:], betas), (bqk_sb[:], bqk), (pe_sb[:], pe),
                  (counts_sb[:], counts), (hid[:, 0, :], tri), (wqkv_sb[:], w_qkv), (rows_sb[:], rows)]
        LATE = [(wo_sb[:], wo), (w1_sb[:], w1), (b1_sb[:], b1), (w2_sb[:], w2), (wa_sb[:], wa),
                (wqk_sb[:], wqk), (rw_sb[:], rw), (tile_no_sb[:], tile_no)]

        @block.sync
        def _(sp):
            sp.dma_start(tok_sb[:], tok).then_inc(tok_in, 16)
            for dst, src in CONSTS:
                sp.dma_start(dst, src).then_inc(consts_in, 16)
            sp.wait_ge(zeros_ready, 2)
            sp.dma_start(regions[E * R:E * R + SPARE * P, :].rearrange("(s p) w -> p s w", p=P),
                         zero_rows[:]).then_inc(spare_out, 16)
            for dst, src in LATE:
                sp.dma_start(dst, src).then_inc(late_in, 16)
            sp.wait_ge(x_ready, 1)
            sp.dma_start(m1_sb[:], m1).then_inc(moe_in, 16)
            sp.dma_start(m2_sb[:], m2).then_inc(moe_in, 16)

            sp.wait_ge(zeros_ready, 4)
            sp.wait_ge(filled_out, 1)
            for e in range(0, E, 2):
                end = sp.value_load(filled_tab[0:1, e:e + 1], min_val=e * R, max_val=e * R + T * P)
                sp.dma_start(regions[bass.ds(end, P), :], zero_rows[:, e, :]).then_inc(zeros_out, 16)

            sp.wait_ge(spare_out, 16)
            sp.wait_ge(scattered, 16 * K * T)
            sp.wait_ge(zeros_out, 16 * E)
            sp.wait_ge(table_ready, 2)

            def load_rows(g, n):
                j = U * g + n
                first = sp.value_load(first_tab[0:1, bass.ds(j, 1)], min_val=0, max_val=E * R + (SPARE - 1) * P)
                if later(g):
                    sp.wait_ge(xe_ps, j - U + 1)
                    sp.wait_ge(dest_ready, j - U + 1)
                sp.dma_start(xr[:, n, :], regions[bass.ds(first, P), :]).then_inc(xr_in[n], 16)

            slot_tiles(sp, load_rows)
            for n in range(U):
                sp.wait_ge(y_out[n], 16 * (SLOTS // U))
            sp.wait_ge(down_ps, SLOTS)

            def load_results(i, b):
                q = YB * i + b
                if later(i):
                    sp.wait_ge(both_added, q - YB + 1)
                for k in range(K):
                    sp.dma_start(yk[b][:, k, :, :], picked[bass.ds(k * T * P + q * (CT * P), CT * P), :].rearrange(
                        "(t p) d -> p t d", p=P)).then_inc(yk_in[b], 16)

            def store_out(q):
                sp.wait_ge(both_added, q + 1)
                sp.dma_start(out[bass.ds(q * CT, CT), :, :].rearrange("t p n -> p t n"),
                             h_all[:, bass.ds(q * CT, CT), :]).then_inc(out_done, 16)

            def load_store(i, b):
                load_results(i, b)
                if later(i) or b >= 2:
                    store_out(YB * i + b - 2)

            sum_steps(sp, load_store)
            for b in range(2):
                store_out(T // CT - 2 + b)
            sp.wait_ge(out_done, 16 * (T // CT))

        @block.gpsimd
        def _(pool):
            pool.memset(half_sb[:], 0.5).then_inc(setup, 1)

            def gather(t):
                if later(t):
                    pool.wait_ge(rows_in, 16 * t)
                    pool.wait_ge(x_ready, t)
                pool.tensor_copy(idx_now[:], tok_sb[:, bass.ds(t, 1)]).then_inc(idx_ready, 1)
                pool.wait_ge(idx_ready, t + 1)
                pool.tensor_tensor(ptick_sb[:, 0:1], half_sb[:], half_sb[:], ALU.add)
                pool.indirect_dma_start(xg[:], None, emb, bass.IndirectOffsetOnAxis(ap=idx_now[:, 0:1], axis=0)
                                        ).then_inc(rows_in, 16)

            pool.wait_ge(setup, 1)
            pool.wait_ge(tok_fixed, 1)
            gather(0)
            pool.memset(mhalf_sb[:], -0.5).then_inc(setup, 1)
            pool.memset(eps_sb[:], EPS_LN).then_inc(setup, 1)
            pool.memset(ones_sb[:], 1.0).then_inc(setup, 1)
            pool.memset(tile_rows_sb[:], float(P)).then_inc(setup, 1)
            pool.memset(vpad[:], 0.0).then_inc(setup, 1)
            pool.memset(kpad[:], 0.0).then_inc(setup, 1)
            pool.memset(qpad[:], 0.0).then_inc(setup, 1)
            pool.memset(zero_rows[:], 0.0).then_inc(setup, 1)
            pool.wait_ge(setup, 9)
            pool.wait_ge(consts_in, 16 * len(CONSTS))
            pool.wait_ge(mask_step, 3)
            pool.tensor_copy(xs[:, :, D:W].rearrange("p k a -> p (k a)"), picked_no).then_inc(zeros_ready, 1)
            pool.tensor_copy(zero_rows[:, :, D:W].rearrange("p s a -> p (s a)"), spare_no).then_inc(zeros_ready, 1)

            def embed(t):
                pool.wait_ge(rows_in, 16 * (t + 1))
                if later(t):
                    pool.wait_ge(xT_ps, t)
                    pool.wait_ge(res_ready, t)
                pool.tensor_tensor(x[:], xg[:], pe_sb[:], ALU.add).then_inc(x_ready, 1)
                pool.wait_ge(x_ready, t + 1)
                pool.tensor_tensor(hrow(t), x[:], row["bo"], ALU.add).then_inc(res_ready, 1)

            def spread_k(t):
                pool.wait_ge(qk_ready, t + 1)
                if later(t):
                    pool.wait_ge(s_ps, t)
                pool.tensor_tensor(kbd[:, 0, :, :], qkT[:, NC:NC + 1, :].broadcast_to([C, HC, P]),
                                   maska_sb[:, :, None].broadcast_to([C, HC, P]), ALU.mult).then_inc(kbd_ready, 1)

            def spread_k2(t):
                pool.wait_ge(qk2_ready, t + 1)
                if later(t):
                    pool.wait_ge(s2_ps, t)
                pool.tensor_tensor(kbd2[:, 0, :, :], qk2T[:, NC:NC + 1, :].broadcast_to([C, HC, P]),
                                   maskb_sb[:, 0, :, None].broadcast_to([C, HC, P]), ALU.mult).then_inc(kbd2_ready, 1)

            def std_tok(t, n):
                pool.wait_ge(mv_ready[n], t + 1)
                pool.tensor_tensor(sd[n][:], mv[n][:, 1:2], half_sb[:], ALU.pow).then_inc(std_ready[n], 1)

            def rstd_plain(t, n):
                pool.wait_ge(mv_ready[n], t + 1)
                if later(t):
                    pool.wait_ge(std_ready[n], t)
                pool.tensor_tensor(sd[n][:], mv[n][:, 1:2], eps_sb[:], ALU.add).then_inc(var_ready[n], 1)
                pool.wait_ge(var_ready[n], t + 1)
                pool.tensor_tensor(rstd[n][:], sd[n][:], mhalf_sb[:], ALU.pow).then_inc(std_ready[n], 1)

            def residual1(t):
                pool.wait_ge(h1_ready, t + 1)
                pool.tensor_tensor(hrow(t), h1[:], row["b2"], ALU.add).then_inc(h1b_ready, 1)

            def norm_hi(t):
                pool.wait_ge(r_ready, t + 1)
                pool.tensor_tensor(prob[:, 8:12, :], prob[:, 8:12, :], rsum[:, 8:12, None].broadcast_to([P, 4, P]),
                                   ALU.mult).then_inc(pn_hi, 1)

            def norm2_hi(t):
                pool.wait_ge(r2_ready, t + 1)
                pool.tensor_tensor(prob2[:, 8:12, :], prob2[:, 8:12, :], rsum2[:, 8:12, None].broadcast_to([P, 4, P]),
                                   ALU.mult).then_inc(pn2_hi, 1)

            def scatter(t, k):
                if k == 0:
                    scatter_ready(t)
                pool.indirect_dma_start(regions, bass.IndirectOffsetOnAxis(ap=slot[k][:, 0:1], axis=0),
                                        xs[:, k, :], None).then_inc(scattered, 16)

            def scatter_ready(t):
                pool.wait_ge(xs_ready, t + 1)
                if later(t):
                    pool.wait_ge(scattered, 16 * K * t)
                pool.tensor_tensor(xs[:, :, D:W].rearrange("p k a -> p (k a)"), xs[:, :, D:W].rearrange(
                    "p k a -> p (k a)"), tile_rows_sb[:], ALU.add).then_inc(ids_ready, 1)
                pool.wait_ge(ids_ready, t + 1)
                pool.wait_ge(slot_ready, K * (t + 1))
                pool.tensor_tensor(ptick_sb[:, 1:2], half_sb[:], half_sb[:], ALU.add)

            def zero_again():
                pool.wait_ge(a_ps, T)
                pool.memset(zero_rows[:], 0.0).then_inc(zeros_ready, 1)
                pool.wait_ge(zeros_ready, 3)
                pool.tensor_copy(zero_rows[:, :, D:W].rearrange("p s a -> p (s a)"), zero_no).then_inc(zeros_ready, 1)

            def body(i):
                at(i, -1, gather)
                at(i, 4, norm2_hi)
                at(i, 0, spread_k)
                at(i, 1, lambda t: std_tok(t, 0))
                at(i, 3, lambda t: std_tok(t, 1))
                if isinstance(i, int) and i == T + SKEW - 1:
                    zero_again()
                at(i, 6, lambda t: scatter(t, 0))
                at(i, 3, lambda t: rstd_plain(t, 2))
                at(i, 6, lambda t: scatter(t, 1))
                at(i, 1, residual1)
                at(i, -1, embed)
                at(i, 3, spread_k2)
                at(i, 0, norm_hi)
                at(i, 4, lambda t: rstd_plain(t, 3))

            embed(0)
            tiles(pool, body)

            def scatter_results(g, n):
                j = U * g + n
                pool.wait_ge(yo_ready, j + 1)
                if later(g):
                    pool.wait_ge(carried, j - U + 1)
                pool.tensor_tensor(ptick_sb[:, 2 + n:3 + n], half_sb[:], half_sb[:],
                                   ALU.add).then_inc(carried, 1)
                pool.indirect_dma_start(picked, bass.IndirectOffsetOnAxis(ap=dest[n][:, 0:1], axis=0),
                                        yo[:, n % 2, :], None).then_inc(y_out[n], 16)

            slot_tiles(pool, scatter_results)

        @block.tensor
        def _(pe_):
            pe_.wait_ge(consts_in, 16 * len(CONSTS))
            pe_.wait_ge(setup, 9)

            def transpose_pair(dst, src):
                for c in range(NC):
                    mm = pe_.transpose(dst[c], src[:, c * C:(c + 1) * C], id_sb[:])
                return mm

            def project(dst, w, xt):
                for n in range(2):
                    for m in range(NC):
                        for k in range(NC):
                            mm = pe_.matmul(dst[:, (NC * n + m) * P:(NC * n + m + 1) * P],
                                            w[:, n, k, m * C:(m + 1) * C], xt[:, k * P:(k + 1) * P],
                                            start=(k == 0), stop=(k == NC - 1))
                return mm

            def scores(dst, qk, kb, first_bank):
                for c, h0, n in ((0, 0, 4), (0, 4, 2), (1, 0, 2), (1, 2, 4)):
                    o = (c * HC + h0) * P
                    mm = pe_.matmul(dst[:, o:o + n * P], qk[:, c, :], kb[:, c, h0:h0 + n, :].rearrange(
                        "p h n -> p (h n)"), start=True, stop=True)
                    if o == 0:
                        mm.then_inc(first_bank, 1)
                return mm

            def split(ap):
                return [ap[:, c * P:(c + 1) * P] for c in range(NC)]

            def a0_xT(t):
                pe_.wait_ge(x_ready, t + 1)
                if later(t):
                    pe_.wait_ge(pT_lo, t)
                transpose_pair(split(XT_A), x).then_inc(xT_ps, 1)

            def a1_qk(t):
                pe_.wait_ge(xT_ready, t + 1)
                if peeled(t) and later(t):
                    pe_.wait_ge(pT_hi, t)
                project(QK_A, wqkv_sb, xT).then_inc(qk_ps, 1)

            def a1_v(t):
                for k in range(NC):
                    mm = pe_.matmul(V_A, xT[:, k * P:(k + 1) * P], wqkv_sb[:, 2, k, :],
                                    start=(k == 0), stop=(k == NC - 1))
                mm.then_inc(v_ps, 1)

            def a2_scores(t):
                if later(t - 5):
                    pe_.wait_ge(filled_ready, t - 5)
                pe_.wait_ge(kbd_ready, t + 1)
                if peeled(t):
                    pe_.wait_ge(kbd_hi, t + 1)
                    pe_.wait_ge(v_ready, t + 1)
                scores(SA, qkT, kbd, s_lo).then_inc(s_ps, 1)

            def a3_probT(t):
                pe_.wait_ge(pn_lo, t + 1)
                for h in range(H):
                    if h == 8:
                        pe_.wait_ge(pn_hi, t + 1)
                    mm = pe_.transpose(SA[:, h * P:(h + 1) * P], prob[:, h, :], id_sb[:])
                    if h == 3:
                        mm.then_inc(pT_bank0, 1)
                    if h == 7:
                        mm.then_inc(pT_bank1, 1)
                mm.then_inc(pT_ps, 1)

            def a4_o(t):
                if peeled(t):
                    pe_.wait_ge(pT_lo, t + 1)
                if later(t - 1):
                    pe_.wait_ge(z_read, t - 1)
                for h in range(H):
                    if h == 4:
                        pe_.wait_ge(pT_mid, t + 1)
                    if h == 8:
                        pe_.wait_ge(pT_hi, t + 1)
                    c, j = divmod(h, HG)
                    mm = pe_.matmul(O_A[G * j:G * j + G, c * P:(c + 1) * P], vpad[:, h, :], probT[:, h, :],
                                    start=True, stop=True)
                mm.then_inc(o_ps, 1)

            def a5_y(t):
                pe_.wait_ge(o_ready, t + 1)
                if later(t):
                    pe_.wait_ge(h1T_ready, t)
                for c in range(NG):
                    mm = pe_.matmul(Y_A, oT[:, c * P:(c + 1) * P], wo_sb[:, c, :], start=(c == 0), stop=(c == NG - 1))
                mm.then_inc(y_ps, 1)

            def a6_h1T(t):
                pe_.wait_ge(h1_ready, t + 1)
                if peeled(t) and later(t):
                    pe_.wait_ge(hid_ready, t)
                transpose_pair(split(H1T_A), h1).then_inc(h1T_ps, 1)

            def a7_ff1(t):
                if peeled(t):
                    pe_.wait_ge(h1T_ready, t + 1)
                    pe_.wait_ge(o_ready, upto(t + 2))
                    if later(t):
                        pe_.wait_ge(z_read, t)
                for m in range(FM):
                    if m == FM // 2:
                        pe_.wait_ge(y_read, upto(t + 2))
                    o = (m % 3) * P
                    dst = (N0 if m < 3 else N1)[:, o:o + P]
                    for k in range(NC):
                        mm = pe_.matmul(dst, w1_sb[:, k, m * P:(m + 1) * P], h1T[:, k * P:(k + 1) * P],
                                        start=(k == 0), stop=(k == NC - 1))
                    if m == 2:
                        mm.then_inc(fa_ps, 1)
                mm.then_inc(fb_ps, 1)

            def a8_ff2(t):
                if peeled(t):
                    pe_.wait_ge(hid_ready, t + 1)
                if later(t - 2):
                    pe_.wait_ge(lgexp_ready, t - 2)
                for m in range(FM):
                    mm = pe_.matmul(Z_A, hid[:, m, :], w2_sb[:, m, :], start=(m == 0), stop=(m == FM - 1))
                mm.then_inc(z_ps, 1)

            def b0_xnT(t):
                pe_.wait_ge(xn_ready, t + 1)
                if later(t):
                    pe_.wait_ge(p2T_hi, t)
                transpose_pair(split(XNT_B), xn).then_inc(xnT_ps, 1)

            def b1_qk(t):
                pe_.wait_ge(xnT_ready, t + 1)
                project(QK_B, wa_sb, xnT).then_inc(qk2_ps, 1)

            def b2_tok(t):
                pe_.wait_ge(qk2_ready, t + 1)
                if peeled(t) and later(t):
                    pe_.wait_ge(aT_ready, t)
                for n in range(2 * NC):
                    mm = pe_.transpose(TOK_B[:, n * C:(n + 1) * C], qk2T[:, n, :], id_sb[0:C, 0:C])
                mm.then_inc(tok_ps, 1)

            def b3_scores(t):
                pe_.wait_ge(kbd2_ready, t + 1)
                if peeled(t):
                    pe_.wait_ge(kbd2_hi, t + 1)
                    pe_.wait_ge(tok_ready, t + 1)
                if later(t):
                    pe_.wait_ge(u_read, t)
                scores(SB, qk2T, kbd2, s2_lo).then_inc(s2_ps, 1)

            def b4_probT(t):
                pe_.wait_ge(pn2_lo, t + 1)
                for h in range(H):
                    if h == 8:
                        pe_.wait_ge(pn2_hi, t + 1)
                    mm = pe_.transpose(SB[:, h * P:(h + 1) * P], prob2[:, h, :], id_sb[:])
                    if h == 3:
                        mm.then_inc(p2T_bank0, 1)
                    if h == 7:
                        mm.then_inc(p2T_bank1, 1)
                mm.then_inc(p2T_ps, 1)

            def b5_a(t):
                if peeled(t):
                    pe_.wait_ge(p2T_hi, t + 1)
                for h in range(H):
                    c, j = divmod(h, HG)
                    dst = A_B[G * j:G * j + G, c * P:(c + 1) * P]
                    pe_.matmul(dst, kpad[:, h, :], prob2T[:, h, :], start=True, stop=False)
                    mm = pe_.matmul(dst, qpad[:, h, :], prob2[:, h, :], start=False, stop=True)
                mm.then_inc(a_ps, 1)

            def b6_u(t):
                pe_.wait_ge(aT_ready, t + 1)
                if peeled(t):
                    pe_.wait_ge(xnT_ready, upto(t + 2))
                for c in range(NG):
                    mm = pe_.matmul(U_B, aT[:, c * P:(c + 1) * P], wqk_sb[:, c, :], start=(c == 0), stop=(c == NG - 1))
                mm.then_inc(u_ps, 1)

            def b7_x2nT(t):
                pe_.wait_ge(x2n_ready, t + 1)
                if peeled(t):
                    pe_.wait_ge(h1T_ready, upto(t + 4))
                    pe_.wait_ge(y_read, upto(t + 5))
                pe_.wait_ge(hid_ready, upto(t + 4))
                transpose_pair(split(X2T_B), x2n).then_inc(x2nT_ps, 1)

            def b8_router(t):
                pe_.wait_ge(x2nT_ready, t + 1)
                if peeled(t):
                    pe_.wait_ge(hid_ready, upto(t + 4))
                    if later(t):
                        pe_.wait_ge(lgexp_ready, t)
                    pe_.wait_ge(z_read, upto(t + 3))
                for k in range(NC):
                    mm = pe_.matmul(LG_B, x2nT[:, k * P:(k + 1) * P], rw_sb[:, k, :],
                                    start=(k == 0), stop=(k == NC - 1))
                mm.then_inc(lg_ps, 1)

            def b9_rank(t):
                if isinstance(t, int) and t == 0:
                    pe_.wait_ge(mask_step, 10)
                pe_.wait_ge(sum_ready, t + 1)
                if peeled(t):
                    pe_.wait_ge(pT_hi, upto(t + 6))
                pe_.matmul(RANK_B, tri_bf[:], chosen_sum[:], start=True, stop=True)
                pe_.matmul(COUNT_B, ones_bf[:], chosen_sum[:], start=True, stop=True).then_inc(rank_ps, 1)

            def body(i):
                if isinstance(i, int) and i == 1:
                    pe_.wait_ge(late_in, 16 * len(LATE))
                at(i, 4, b3_scores)
                at(i, 1, a3_probT)
                at(i, 0, a0_xT)
                at(i, 2, a6_h1T)
                at(i, 1, a4_o)
                at(i, 0, a1_qk)
                at(i, 6, b9_rank)
                at(i, 0, a1_v)
                at(i, 1, a5_y)
                at(i, 2, a7_ff1)
                at(i, 4, b4_probT)
                at(i, 5, b7_x2nT)
                at(i, 0, a2_scores)
                at(i, 5, b8_router)
                at(i, 3, b0_xnT)
                at(i, 4, b5_a)
                at(i, 3, b1_qk)
                at(i, 4, b6_u)
                at(i, 3, b2_tok)
                at(i, 2, a8_ff2)

            tiles(pe_, body)

            pe_.wait_ge(imp_ready, 1)
            pe_.matmul(IMP, ones_sb[:], imp[:], start=True, stop=True).then_inc(imp_ps, 1)
            pe_.wait_ge(moe_in, 32)
            pe_.wait_ge(imp_read, 1)
            pe_.wait_ge(table_ready, 2)

            def rows_T(g, n):
                j = U * g + n
                pe_.wait_ge(xr_in[n], 16 * (g + 1))
                if later(j - 1):
                    pe_.wait_ge(xe_ready, j - 1)
                transpose_pair(split(ps[0:C, 4 + n % 2, 0:NC * P]), xr[:, n, 0:D]).then_inc(xe_ps, 1)

            def experts_of(first, n):
                return nc.values_load_multi_w_load_instructions(
                    expert_tab[0:1, bass.ds(first, n)], engines=(mybir.EngineType.PE,), min_val=0, max_val=E - 1)[1]

            def up(g, n, e):
                j = U * g + n
                pe_.wait_ge(xe_ready, j + 1)
                if later(j - 1):
                    pe_.wait_ge(eh_ready, j - 1)
                for k in range(NC):
                    mm = pe_.matmul(ps[:, n % 2, :], xeT[:, n % 2, k * P:(k + 1) * P],
                                    m1_sb[:, k, bass.ds(e * EI, EI)], start=(k == 0), stop=(k == NC - 1))
                mm.then_inc(up_ps, 1)

            def hidden_T(g, n):
                j = U * g + n
                pe_.wait_ge(eh_ready, j + 1)
                if later(j - 1):
                    pe_.wait_ge(ehT_ready, j - 1)
                for m in range(EM):
                    mm = pe_.transpose(ps[:, 2 + n % 2, m * P:(m + 1) * P], ehid[:, n % 2, m * P:(m + 1) * P], id_sb[:])
                mm.then_inc(ehT_ps, 1)

            def down(g, n, e):
                j = U * g + n
                pe_.wait_ge(ehT_ready, j + 1)
                if later(j - 1):
                    pe_.wait_ge(yo_ready, j - 1)
                for m in range(EM):
                    mm = pe_.matmul(ps[:, 6 + n % 2, 0:D], ehT[:, n % 2, m * P:(m + 1) * P],
                                    m2_sb[:, m, bass.ds(e, 1), :].rearrange("p a d -> p (a d)"),
                                    start=(m == 0), stop=(m == EM - 1))
                mm.then_inc(down_ps, 1)

            def shifted_by(stage, g, n, back):
                g, n = g + (n - back) // U, (n - back) % U
                if not isinstance(g, int) or 0 <= g < SLOTS // U:
                    stage(g, n)

            loaded = {}

            def expert_step(g, n):
                if n == 0:
                    first = -2 if later(g) else 0
                    loaded.clear()
                    loaded.update(enumerate(experts_of(U * g + first, U - first), first))
                up(g, n, loaded[n])
                shifted_by(rows_T, g, n, -1)
                shifted_by(hidden_T, g, n, 1)
                shifted_by(lambda g, m: down(g, m, loaded[n - 2]), g, n, 2)

            rows_T(0, 0)
            slot_tiles(pe_, expert_step)
            hidden_T(SLOTS // U - 1, U - 1)
            down(SLOTS // U - 1, U - 2, loaded[U - 2])
            down(SLOTS // U - 1, U - 1, loaded[U - 1])

        @block.scalar
        def _(act):
            act.wait_ge(consts_in, 16 * len(CONSTS))
            act.wait_ge(zeros_ready, 2)
            act.wait_ge(spare_out, 16)

            def copy(dst, src):
                return act.activation(dst, src, ACT.Copy)

            def c_xT(t):
                act.wait_ge(xT_ps, t + 1)
                if later(t):
                    act.wait_ge(v_ps, t)
                copy(xT[:], XT_A).then_inc(xT_ready, 1)

            def exponentials(part, src, dst, nm, ls):
                for h in range(4 * part, 4 * part + 4):
                    a = act.activation(dst[:, h, :], src[:, h * P:(h + 1) * P], ACT.Exp, bias=nm[:, h:h + 1],
                                       accum_out=ls[:, h:h + 1])
                return a

            def c_exp(part):
                def stage(t):
                    if part == 0:
                        if later(t):
                            act.wait_ge(pT_ps, t)
                            act.wait_ge(r_ready, t)
                        act.wait_ge(nm_lo, t + 1)
                    if part == 1:
                        act.wait_ge(nm_ready, t + 1)
                    a = exponentials(part, SA, prob, nmax, lsum)
                    if part == 1:
                        a.then_inc(p_lo, 1)
                    if part == 2:
                        a.then_inc(p_ready, 1)
                return stage

            def c_exp2(part):
                def stage(t):
                    if part == 0:
                        if later(t):
                            act.wait_ge(a_ps, t)
                            act.wait_ge(r2_ready, t)
                        act.wait_ge(nm2_lo, t + 1)
                    if part == 1:
                        act.wait_ge(nm2_ready, t + 1)
                    a = exponentials(part, SB, prob2, nmax2, lsum2)
                    if part == 1:
                        a.then_inc(p2_lo, 1)
                    if part == 2:
                        a.then_inc(p2_ready, 1)
                return stage

            def c_pT(t):
                act.wait_ge(pT_bank0, t + 1)
                if later(t):
                    act.wait_ge(o_ps, t)
                copy(probT[:, 0:4, :].rearrange("p h n -> p (h n)"), SA[:, 0:512]).then_inc(pT_lo, 1)
                act.wait_ge(pT_bank1, t + 1)
                copy(probT[:, 4:8, :].rearrange("p h n -> p (h n)"), SA[:, 512:1024]).then_inc(pT_mid, 1)
                act.wait_ge(pT_ps, t + 1)
                copy(probT[:, 8:12, :].rearrange("p h n -> p (h n)"), SA[:, 1024:1536]).then_inc(pT_hi, 1)

            def c_p2T(t):
                act.wait_ge(p2T_bank0, t + 1)
                if later(t):
                    act.wait_ge(a_ps, t)
                copy(prob2T[:, 0:4, :].rearrange("p h n -> p (h n)"), SB[:, 0:512])
                act.wait_ge(p2T_bank1, t + 1)
                copy(prob2T[:, 4:8, :].rearrange("p h n -> p (h n)"), SB[:, 512:1024])
                act.wait_ge(p2T_ps, t + 1)
                copy(prob2T[:, 8:12, :].rearrange("p h n -> p (h n)"), SB[:, 1024:1536]).then_inc(p2T_hi, 1)

            def c_x2nT(t):
                act.wait_ge(x2nT_ps, t + 1)
                if later(t):
                    act.wait_ge(lg_ps, t)
                copy(x2nT[:], X2T_B).then_inc(x2nT_ready, 1)

            def c_o(t):
                act.wait_ge(o_ps, t + 1)
                if later(t):
                    act.wait_ge(y_ps, t)
                copy(oT[:], O_A).then_inc(o_ready, 1)

            def c_h1T(t):
                act.wait_ge(h1T_ps, t + 1)
                if later(t):
                    act.wait_ge(fb_ps, t)
                copy(h1T[:], H1T_A).then_inc(h1T_ready, 1)

            def c_hid(t):
                act.wait_ge(fa_ps, t + 1)
                if later(t):
                    act.wait_ge(z_ps, t)
                for m in range(FM):
                    if m == FM // 2:
                        act.wait_ge(fb_ps, t + 1)
                    src = (N0 if m < FM // 2 else N1)[:, (m % 3) * P:(m % 3 + 1) * P]
                    a = act.activation(hid[:, m, :], src, ACT.Relu, bias=b1_sb[:, m:m + 1])
                a.then_inc(hid_ready, 1)

            def c_xnT(t):
                act.wait_ge(xnT_ps, t + 1)
                if later(t):
                    act.wait_ge(qk2_ps, t)
                copy(xnT[:], XNT_B).then_inc(xnT_ready, 1)

            def c_aT(t):
                act.wait_ge(a_ps, t + 1)
                if later(t):
                    act.wait_ge(u_ps, t)
                copy(aT[:], A_B).then_inc(aT_ready, 1)

            def c_lg(t):
                act.wait_ge(lgmax_ready, t + 1)
                if later(t):
                    act.wait_ge(route_ready, t)
                act.activation(lg[:], LG_B, ACT.Exp, bias=lgmax[:], accum_out=lgsum[:]).then_inc(lgexp_ready, 1)

            def c_xs(t):
                act.wait_ge(x2n_ready, t + 1)
                if later(t):
                    act.wait_ge(scattered, 16 * K * t)
                copy(xs[:, :, 0:D], x2n[:, None, :].broadcast_to([P, K, D])).then_inc(xs_ready, 1)

            def body(i):
                if isinstance(i, int) and i == 1:
                    act.wait_ge(late_in, 16 * len(LATE))
                at(i, 4, c_exp2(0))
                at(i, 1, c_pT)
                at(i, 0, c_xT)
                at(i, 2, c_h1T)
                at(i, 4, c_exp2(1))
                at(i, 1, c_o)
                at(i, 4, c_exp2(2))
                at(i, 2, c_hid)
                at(i, 4, c_p2T)
                at(i, 5, c_x2nT)
                at(i, 3, c_xnT)
                at(i, 0, c_exp(0))
                at(i, 5, c_lg)
                at(i, 4, c_aT)
                at(i, 5, c_xs)
                at(i, 0, c_exp(1))
                at(i, 0, c_exp(2))

            tiles(act, body)

            def evacuate_rows(g, n):
                j = U * g + n
                act.wait_ge(xe_ps, j + 1)
                if later(j - 1):
                    act.wait_ge(up_ps, j - 1)
                copy(xeT[:, n % 2, :], ps[0:C, 4 + n % 2, 0:NC * P]).then_inc(xe_ready, 1)

            def expert_step(g, n):
                j = U * g + n
                act.wait_ge(up_ps, j + 1)
                if later(j - 1):
                    act.wait_ge(ehT_ps, j - 1)
                act.activation(ehid[:, n % 2, :], ps[:, n % 2, :], ACT.Silu).then_inc(eh_ready, 1)
                g, n = g + (n + 1) // U, (n + 1) % U
                if not isinstance(g, int) or g < SLOTS // U:
                    evacuate_rows(g, n)

            act.wait_ge(zeros_ready, 4)
            act.wait_ge(filled_out, 1)
            for e in range(1, E, 2):
                end = act.value_load(filled_tab[0:1, e:e + 1], min_val=e * R, max_val=e * R + T * P)
                act.dma_start(regions[bass.ds(end, P), :], zero_rows[:, e, :]).then_inc(zeros_out, 16)

            act.wait_ge(table_ready, 2)
            evacuate_rows(0, 0)
            slot_tiles(act, expert_step)

        @block.vector
        def _(dve):
            dve.wait_ge(tok_in, 16)
            dve.tensor_scalar(neg_sb[:], tok_sb[:], 0.0, float(V), ALU.is_lt, ALU.mult).then_inc(tok_step, 1)
            dve.wait_ge(tok_step, 1)
            dve.tensor_tensor(tok_sb[:], tok_sb[:], neg_sb[:], ALU.add).then_inc(tok_step, 1)
            dve.wait_ge(tok_step, 2)
            dve.tensor_scalar(tok_sb[:], tok_sb[:], 0.0, float(V - 1), ALU.max, ALU.min).then_inc(tok_fixed, 1)
            dve.wait_ge(consts_in, 16 * len(CONSTS))
            dve.wait_ge(setup, 9)
            dve.tensor_scalar(maska_sb[:], mask_sb[:], float(HD) ** -0.5, None, ALU.mult).then_inc(mask_step, 1)
            for c in range(NC):
                dve.tensor_scalar(maskb_sb[:, c, :], mask_sb[:], betas_sb[:, c:c + 1], None,
                                  ALU.mult).then_inc(mask_step, 1)
            dve.tensor_copy(filled[:], region_no).then_inc(mask_step, 1)
            dve.tensor_copy(tri_bf[:], hid[:, 0, :]).then_inc(mask_step, 1)
            dve.tensor_copy(ones_bf[:], ones_sb[:]).then_inc(mask_step, 1)
            for n in range(4):
                dve.memset(until[n][:], 0.0).then_inc(mask_step, 1)
            dve.wait_ge(mask_step, 10)

            ticks = [0]

            def tick():
                k = ticks[0] = (ticks[0] + 1) % 16
                dve.memset(tick_sb[:, k:k + 1], 0.0)

            def v_qk(t):
                dve.wait_ge(qk_ps, t + 1)
                if later(t):
                    dve.wait_ge(s_ps, t)
                dve.tensor_tensor(qkT[:], QK_A.rearrange("p (n k) -> p n k", n=2 * NC),
                                  bqk_sb[:, :, None].broadcast_to([C, 2 * NC, P]), ALU.add).then_inc(qk_ready, 1)
                dve.wait_ge(v_ps, t + 1)
                if later(t):
                    dve.wait_ge(o_ps, t)
                dve.tensor_tensor(vpad[:, :, 0:HD], V_A.rearrange("p (h d) -> p h d", h=H),
                                  row["bv"].rearrange("p (h d) -> p h d", h=H), ALU.add).then_inc(v_ready, 1)

            def v_spread_k(t):
                dve.wait_ge(qk_ready, t + 1)
                if later(t):
                    dve.wait_ge(s_ps, t)
                dve.tensor_tensor(kbd[:, 1, :, :], qkT[:, NC + 1:NC + 2, :].broadcast_to([C, HC, P]),
                                  maska_sb[:, :, None].broadcast_to([C, HC, P]), ALU.mult).then_inc(kbd_hi, 1)

            def v_max(t):
                if later(t):
                    dve.wait_ge(p_ready, t)
                dve.wait_ge(s_lo, t + 1)
                dve.tensor_reduce(nmax[:, 0:4], SA[:, 0:512].rearrange("p (h n) -> p h n", h=4), AX.X, ALU.max,
                                  negate=True).then_inc(nm_lo, 1)
                dve.wait_ge(s_ps, t + 1)
                dve.tensor_reduce(nmax[:, 4:12], SA[:, 512:1536].rearrange("p (h n) -> p h n", h=8), AX.X, ALU.max,
                                  negate=True).then_inc(nm_ready, 1)

            def v_max2(t):
                if later(t):
                    dve.wait_ge(p2_ready, t)
                dve.wait_ge(s2_lo, t + 1)
                dve.tensor_reduce(nmax2[:, 0:4], SB[:, 0:512].rearrange("p (h n) -> p h n", h=4), AX.X, ALU.max,
                                  negate=True).then_inc(nm2_lo, 1)
                yield
                yield
                dve.wait_ge(s2_ps, t + 1)
                dve.tensor_reduce(nmax2[:, 4:12], SB[:, 512:1536].rearrange("p (h n) -> p h n", h=8), AX.X, ALU.max,
                                  negate=True).then_inc(nm2_ready, 1)

            def v_norm(t):
                if later(t):
                    dve.wait_ge(pn_lo, t)
                    dve.wait_ge(pn_hi, t)
                dve.wait_ge(p_lo, t + 1)
                dve.reciprocal(rsum[:, 0:8], lsum[:, 0:8]).then_inc(r_lo, 1)
                dve.wait_ge(r_lo, t + 1)
                dve.tensor_tensor(prob[:, 0:8, :], prob[:, 0:8, :], rsum[:, 0:8, None].broadcast_to([P, 8, P]),
                                  ALU.mult).then_inc(pn_lo, 1)
                dve.wait_ge(p_ready, t + 1)
                dve.reciprocal(rsum[:, 8:12], lsum[:, 8:12]).then_inc(r_ready, 1)

            def v_norm2(t):
                if later(t):
                    dve.wait_ge(pn2_lo, t)
                    dve.wait_ge(pn2_hi, t)
                dve.wait_ge(p2_lo, t + 1)
                dve.reciprocal(rsum2[:, 0:8], lsum2[:, 0:8]).then_inc(r2_lo, 1)
                dve.wait_ge(r2_lo, t + 1)
                dve.tensor_tensor(prob2[:, 0:8, :], prob2[:, 0:8, :], rsum2[:, 0:8, None].broadcast_to([P, 8, P]),
                                  ALU.mult).then_inc(pn2_lo, 1)
                dve.wait_ge(p2_ready, t + 1)
                dve.reciprocal(rsum2[:, 8:12], lsum2[:, 8:12]).then_inc(r2_ready, 1)

            def stats(n, t, src):
                tick()
                dve.bn_stats(st[n][:], src).then_inc(st_ready[n], 1)
                yield
                dve.wait_ge(st_ready[n], t + 1)
                tick()
                dve.bn_aggr(mv[n][:], st[n][:]).then_inc(mv_ready[n], 1)
                yield
                dve.wait_ge(mv_ready[n], t + 1)

            def tok_norm(n, t, src, tmp, gamma):
                dve.scalar_tensor_tensor(tmp, src, mv[n][:, 0:1], gamma, ALU.subtract, ALU.mult).then_inc(shifted[n], 1)
                yield
                dve.wait_ge(std_ready[n], t + 1)
                dve.tensor_scalar(sd[n][:], sd[n][:], EPS_TOK, None, ALU.add).then_inc(sd_ready[n], 1)
                yield
                dve.wait_ge(sd_ready[n], t + 1)
                dve.reciprocal(rstd[n][:], sd[n][:]).then_inc(rstd_ready[n], 1)
                yield
                dve.wait_ge(rstd_ready[n], t + 1)
                dve.wait_ge(shifted[n], t + 1)

            def v_y(t):
                dve.wait_ge(y_ps, t + 1)
                dve.wait_ge(res_ready, t + 1)
                dve.tensor_tensor(y[:], Y_A, hrow(t), ALU.add).then_inc(y_read, 1)
                yield
                dve.wait_ge(y_read, t + 1)
                yield from stats(0, t, y[:])
                yield from tok_norm(0, t, y[:], yc[:], row["gamma1"])
                if later(t):
                    dve.wait_ge(h1T_ps, t)
                    dve.wait_ge(h1b_ready, t)
                dve.scalar_tensor_tensor(h1[:], yc[:], rstd[0][:], row["beta1"], ALU.mult,
                                         ALU.add).then_inc(h1_ready, 1)

            def v_zread(t):
                dve.wait_ge(z_ps, t + 1)
                dve.wait_ge(h1b_ready, t + 1)
                dve.tensor_tensor(z[:], Z_A, hrow(t), ALU.add).then_inc(z_read, 1)

            def v_z(t):
                dve.wait_ge(z_read, t + 1)
                yield from stats(1, t, z[:])
                yield from tok_norm(1, t, z[:], zc[:], row["gamma2"])
                dve.scalar_tensor_tensor(hs[:], zc[:], rstd[1][:], row["beta2"], ALU.mult,
                                         ALU.add).then_inc(hs_ready, 1)
                yield
                dve.wait_ge(hs_ready, t + 1)
                yield from stats(2, t, hs[:])
                tick()
                dve.tensor_copy(hrow(t), hs[:]).then_inc(h_ready, 1)

            def v_xn(t):
                dve.wait_ge(std_ready[2], t + 1)
                if later(t):
                    dve.wait_ge(xnT_ps, t)
                dve.tensor_scalar(xn[:], hs[:], mv[2][:, 0:1], rstd[2][:], ALU.subtract,
                                  ALU.mult).then_inc(xn_ready, 1)

            def v_u(t):
                dve.wait_ge(u_ps, t + 1)
                dve.wait_ge(h_ready, t + 1)
                dve.tensor_tensor(h2[:], U_B, hrow(t), ALU.add).then_inc(u_read, 1)

            def v_h2(t):
                dve.wait_ge(u_read, t + 1)
                yield from stats(3, t, h2[:])
                tick()
                dve.tensor_copy(hrow(t), h2[:])

            def v_x2n(t):
                dve.wait_ge(std_ready[3], t + 1)
                if later(t):
                    dve.wait_ge(x2nT_ps, t)
                    dve.wait_ge(xs_ready, t)
                dve.tensor_scalar(x2n[:], h2[:], mv[3][:, 0:1], rstd[3][:], ALU.subtract,
                                  ALU.mult).then_inc(x2n_ready, 1)

            def in_turns(*stages):
                stages = list(stages)
                while stages:
                    stages = [g for g in stages if next(g, stages) is not stages]

            def v_tok(t):
                dve.wait_ge(tok_ps, t + 1)
                if later(t):
                    dve.wait_ge(a_ps, t)
                dve.tensor_copy(qpad[:, :, HD:G], TOK_B[:, 0:D].rearrange("p (h d) -> p h d", h=H))
                dve.tensor_copy(kpad[:, :, 0:HD], TOK_B[:, D:2 * D].rearrange("p (h d) -> p h d", h=H)
                                ).then_inc(tok_ready, 1)

            def v_qk2(t):
                dve.wait_ge(qk2_ps, t + 1)
                if later(t):
                    dve.wait_ge(s2_ps, t)
                dve.tensor_copy(qk2T[:].rearrange("p n k -> p (n k)"), QK_B).then_inc(qk2_ready, 1)

            def v_spread_k2(t):
                dve.wait_ge(qk2_ready, t + 1)
                dve.tensor_tensor(kbd2[:, 1, :, :], qk2T[:, NC + 1:NC + 2, :].broadcast_to([C, HC, P]),
                                  maskb_sb[:, 1, :, None].broadcast_to([C, HC, P]), ALU.mult).then_inc(kbd2_hi, 1)

            def v_lgmax(t):
                dve.wait_ge(lg_ps, t + 1)
                dve.tensor_reduce(lgmax[:], LG_B, AX.X, ALU.max, negate=True).then_inc(lgmax_ready, 1)

            def v_probs(t):
                dve.wait_ge(lgexp_ready, t + 1)
                dve.reciprocal(lginv[:], lgsum[:]).then_inc(lginv_ready, 1)
                yield
                dve.wait_ge(lginv_ready, t + 1)
                dve.tensor_scalar(pr[:], lg[:], lginv[:], None, ALU.mult).then_inc(pr_ready, 1)
                yield
                dve.wait_ge(pr_ready, t + 1)
                tick()
                dve.tensor_copy(probs_all[:, bass.ds(t, 1), :].rearrange("p a e -> p (a e)"), pr[:])
                dve.max(top8[:], pr[:]).then_inc(top8_ready, 1)
                yield
                dve.wait_ge(top8_ready, t + 1)
                tick()
                dve.max_index(idx8[:], top8[:], pr[:]).then_inc(idx8_ready, 1)
                yield
                dve.wait_ge(idx8_ready, t + 1)
                dve.tensor_copy(route[:, K:2 * K], idx8[:, 0:K])
                dve.tensor_copy(route[:, 0:K], top8[:, 0:K]).then_inc(route_ready, 1)
                yield
                dve.wait_ge(route_ready, t + 1)
                tick()
                dve.tensor_copy(route_all[:, bass.ds(t, 1), :].rearrange("p a e -> p (a e)"), route[:])
                dve.tensor_tensor(chosen[:], route[:, K:2 * K, None].broadcast_to([P, K, E]),
                                  expert_no[:, None, :].broadcast_to([P, K, E]), ALU.is_equal).then_inc(chosen_ready, 1)
                yield
                dve.wait_ge(chosen_ready, t + 1)
                dve.tensor_tensor(chosen_sum[:], chosen[:, 0, :], chosen[:, 1, :], ALU.add).then_inc(sum_ready, 1)

            def v_slots(t):
                dve.wait_ge(rank_ps, t + 1)
                if later(t):
                    dve.wait_ge(filled_ready, t)
                dve.tensor_tensor(place[:], RANK_B, filled[:], ALU.add).then_inc(place_ready, 1)
                dve.tensor_tensor(filled[:], COUNT_B, filled[:], ALU.add).then_inc(filled_ready, 1)
                yield
                dve.wait_ge(place_ready, t + 1)
                dve.tensor_tensor(placed[:], chosen[:], place[:, None, :].broadcast_to([P, K, E]),
                                  ALU.mult).then_inc(placed_ready, 1)
                yield
                dve.wait_ge(placed_ready, t + 1)
                dve.tensor_reduce(slotf[:], placed[:], AX.X, ALU.add).then_inc(slotf_ready, 1)
                yield
                dve.wait_ge(slotf_ready, t + 1)
                if later(t):
                    dve.wait_ge(scattered, 16 * K * t)
                for k in range(K):
                    dve.tensor_copy(slot[k][:], slotf[:, k:k + 1]).then_inc(slot_ready, 1)

            def tile_stage(i, skew, stage):
                if isinstance(i, int) and not 0 <= i - skew < T:
                    return iter(())
                return stage(i - skew)

            def body(i):
                at(i, 4, v_norm2)
                at(i, 0, v_qk)
                at(i, 0, v_spread_k)
                in_turns(tile_stage(i, 1, v_y), tile_stage(i, 6, v_slots), tile_stage(i, 3, v_z))
                at(i, 3, v_xn)
                at(i, 0, v_max)
                at(i, 5, v_lgmax)
                at(i, 3, v_qk2)
                at(i, 3, v_spread_k2)
                at(i, 3, v_tok)
                at(i, 4, v_u)
                at(i, 0, v_norm)
                at(i, 2, v_zread)
                in_turns(tile_stage(i, 3, v_max2), tile_stage(i, 4, v_h2), tile_stage(i, 5, v_probs))
                if isinstance(i, int) and i == T + 4:
                    dve.wait_ge(sum_ready, T)
                    dve.tensor_reduce(imp[:], probs_all[:].rearrange("p t e -> p e t"), AX.X,
                                      ALU.add).then_inc(imp_ready, 1)
                at(i, 4, v_x2n)

            tiles(dve, body)

            dve.wait_ge(filled_ready, T)
            dve.tensor_copy(filled_tab[:], filled[0:1, :]).then_inc(filled_out, 1)
            dve.tensor_tensor(step_of[:], filled[:], region_no, ALU.subtract).then_inc(table_step, 1)
            dve.wait_ge(table_step, 1)
            dve.tensor_scalar(step_of[:], step_of[:], float(P - 1), 1.0 / P, ALU.add, ALU.mult).then_inc(table_step, 1)
            dve.wait_ge(table_step, 2)
            dve.tensor_scalar(step_of[:], step_of[:], -(P - 1) / (2.0 * P), 2.0 ** 23, ALU.add,
                              ALU.add).then_inc(table_step, 1)
            dve.wait_ge(table_step, 3)
            dve.tensor_scalar(until[0][:, E:], step_of[:], -2.0 ** 23, None, ALU.add).then_inc(table_step, 1)
            dve.wait_ge(table_step, 4)
            for n in range(3):
                dve.tensor_tensor(until[n + 1][:, E:], until[n][:, E:], until[n][:, E - 2 ** n:2 * E - 2 ** n],
                                  ALU.add).then_inc(table_step, 1)
                dve.wait_ge(table_step, 5 + n)
            dve.wait_ge(late_in, 16 * len(LATE))
            tile_b = tile_no_sb[0:1, :, None].broadcast_to([1, SLOTS, E])
            dve.tensor_tensor(before, tile_b, until[3][0:1, None, E:].broadcast_to([1, SLOTS, E]),
                              ALU.is_ge).then_inc(table_step, 1)
            dve.tensor_scalar(step_of[:], until[0][:, E:], -float(P), float(R), ALU.mult,
                              ALU.add).then_inc(table_step, 1)
            dve.wait_ge(table_step, 9)
            dve.tensor_tensor(steps, before, step_of[0:1, None, :].broadcast_to([1, SLOTS, E]),
                              ALU.mult).then_inc(table_step, 1)
            dve.tensor_reduce(expert_f, before, AX.X, ALU.add).then_inc(table_step, 1)
            dve.wait_ge(table_step, 10)
            dve.tensor_reduce(first_f, steps, AX.X, ALU.add).then_inc(table_step, 1)
            dve.wait_ge(table_step, 11)
            dve.tensor_scalar(expert_tab[:], expert_f, float(E - 1), None, ALU.min).then_inc(table_ready, 1)
            dve.wait_ge(table_step, 12)
            dve.scalar_tensor_tensor(first_tab[:], tile_no_sb[:], float(P), first_f, ALU.mult,
                                     ALU.add).then_inc(table_ready, 1)

            dve.wait_ge(imp_ps, 1)
            dve.tensor_scalar(rinv[:], IMP, -1.0, 1.0 - 0.9, ALU.add, ALU.mult).then_inc(imp_read, 1)
            dve.wait_ge(imp_read, 1)
            dve.tensor_scalar(rinv[:], rinv[:], 1.0, 0.01, ALU.add, ALU.add).then_inc(share_step, 1)
            dve.wait_ge(share_step, 1)
            dve.reciprocal(rinv[:], rinv[:]).then_inc(share_step, 1)
            for k in range(K):
                dve.wait_ge(share_step, 2 + 4 * k)
                dve.tensor_tensor(bal, route_all[:, :, K + k:K + k + 1].broadcast_to([P, T, E]),
                                  expert_no[:, None, :].broadcast_to([P, T, E]), ALU.is_equal).then_inc(share_step, 1)
                dve.wait_ge(share_step, 3 + 4 * k)
                dve.tensor_tensor(bal, bal, rinv[:, None, :].broadcast_to([P, T, E]), ALU.mult).then_inc(share_step, 1)
                dve.wait_ge(share_step, 4 + 4 * k)
                dve.tensor_reduce(share[:, :, k:k + 1].rearrange("p t a -> p (t a)"), bal, AX.X,
                                  ALU.add).then_inc(share_step, 1)
                dve.wait_ge(share_step, 5 + 4 * k)
                dve.tensor_tensor(share[:, :, k:k + 1], share[:, :, k:k + 1], route_all[:, :, k:k + 1],
                                  ALU.mult).then_inc(share_step, 1)
            dve.wait_ge(share_step, 10)
            dve.tensor_reduce(csum[:], share[:], AX.X, ALU.add).then_inc(share_step, 1)
            dve.wait_ge(share_step, 11)
            dve.reciprocal(csum[:], csum[:]).then_inc(share_step, 1)
            dve.wait_ge(share_step, 12)
            dve.tensor_tensor(share[:], share[:], csum[:, :, None].broadcast_to([P, T, K]),
                              ALU.mult).then_inc(share_step, 1)

            def rows_dest(g, n):
                j = U * g + n
                dve.wait_ge(xr_in[n], 16 * (g + 1))
                if later(g):
                    dve.wait_ge(y_out[n], 16 * g)
                dve.tensor_copy(dest[n][:], xr[:, n, D:W]).then_inc(dest_ready, 1)

            def evacuate_hidden(g, n):
                j = U * g + n
                dve.wait_ge(ehT_ps, j + 1)
                if later(j - 1):
                    dve.wait_ge(down_ps, j - 1)
                dve.tensor_copy(ehT[:, n % 2, :], ps[:, 2 + n % 2, :]).then_inc(ehT_ready, 1)

            def evacuate_results(g, n):
                j = U * g + n
                dve.wait_ge(down_ps, j + 1)
                dve.wait_ge(dest_ready, j + 1)
                if later(j - 1):
                    dve.wait_ge(y_out[(n - 2) % U], 16 * (g + (n - 2) // U + 1))
                dve.tensor_copy(yo[:, n % 2, :], ps[:, 6 + n % 2, 0:D]).then_inc(yo_ready, 1)

            def shifted_by(stage, g, n, back):
                g, n = g + (n - back) // U, (n - back) % U
                if not isinstance(g, int) or 0 <= g < SLOTS // U:
                    stage(g, n)

            def expert_step(g, n):
                rows_dest(g, n)
                shifted_by(evacuate_hidden, g, n, 1)
                shifted_by(evacuate_results, g, n, 2)

            slot_tiles(dve, expert_step)
            evacuate_hidden(SLOTS // U - 1, U - 1)
            evacuate_results(SLOTS // U - 1, U - 2)
            evacuate_results(SLOTS // U - 1, U - 1)
            dve.wait_ge(share_step, 13)

            def add_results(i, b):
                q = YB * i + b
                dve.wait_ge(yk_in[b], 32 * (i + 1))
                for k in range(K):
                    if k == 1:
                        dve.wait_ge(first_added, q + 1)
                    for c in range(CT):
                        w = share[:, bass.ds(q * CT + c, 1), k:k + 1].rearrange("p a n -> p (a n)")
                        a = dve.scalar_tensor_tensor(hrow(q * CT + c), yk[b][:, k, c, :], w, hrow(q * CT + c),
                                                     ALU.mult, ALU.add)
                    a.then_inc(first_added if k == 0 else both_added, 1)

            sum_steps(dve, add_results)


def position_table():
    import numpy as np
    pos = np.arange(P, dtype=np.float32)[:, None]
    i = np.arange(D, dtype=np.float32)[None, :]
    ang = pos / np.power(np.float32(10000.0), np.float32(2.0) * i / np.float32(D))
    return np.where((np.arange(D) % 2 == 0)[None, :], np.cos(ang), np.sin(ang)).astype(np.float32)


def counting():
    import numpy as np
    p = np.arange(P, dtype=np.float32)[:, None]
    columns = [np.arange(E), R * np.arange(E)]
    columns = [np.broadcast_to(c.astype(np.float32), (P, E)) for c in columns]
    columns.append(p + T * P * np.arange(K, dtype=np.float32) - P)
    columns.append(p + PICKED + P * np.arange(2 * SPARE, dtype=np.float32))
    return np.concatenate(columns, 1).astype(np.float32)


def lay_out(a):
    import numpy as np

    def chunks(w, rows):
        return w.reshape(w.shape[0] // rows, rows, -1).transpose(1, 0, 2)

    def heads(first, second):
        w = np.zeros((H, 2, HD, D), np.float32)
        w[:, 0] = first.reshape(H, HD, D)
        if second is not None:
            w[:, 1] = second.reshape(H, HD, D)
        return chunks(w.reshape(H * G, D), P)

    row_names = [a["L0_tok_" + n] for n in ROWS]
    return {
        "tok": a["x"].T,
        "emb": a["L0_tok_emb"],
        "pe": position_table(),
        "ident": np.eye(P, dtype=np.float32),
        "hmask": (np.arange(C)[:, None] // HD == np.arange(HC)[None, :]).astype(np.float32),
        "w_qkv": np.stack([chunks(a["L0_tok_" + n], C) for n in ("wq", "wk", "wv")], 1),
        "bqk": np.concatenate([a["L0_tok_bq"].reshape(NC, C), a["L0_tok_bk"].reshape(NC, C)]).T,
        "rows": np.broadcast_to(np.stack(row_names)[None], (P, len(ROWS), D)),
        "wo": heads(a["L0_tok_wo"], None),
        "w1": chunks(a["L0_tok_w1"], C),
        "b1": a["L0_tok_b1"].reshape(FM, P).T,
        "w2": chunks(a["L0_tok_w2"], P),
        "wa": np.stack([chunks(a["L0_attn_Wq"].T, C), chunks(a["L0_attn_Wk"].T, C)], 1),
        "betas": np.repeat(a["L0_attn_betas"], HD).reshape(NC, C).T,
        "wqk": heads(a["L0_attn_Wq"], a["L0_attn_Wk"]),
        "rw": chunks(a["L0_ffn_router_w"].T, C),
        "m1": chunks(a["L0_ffn_w1"].transpose(2, 0, 1).reshape(D, E * EI), C),
        "m2": a["L0_ffn_w2"].transpose(2, 0, 1).reshape(EM, P, E, D).transpose(1, 0, 2, 3),
        "tri": (np.arange(P)[:, None] < np.arange(P)[None, :]).astype(np.float32),
        "counts": counting(),
        "tile_no": np.arange(SLOTS, dtype=np.float32)[None, :],
    }


def kernel(**inputs):
    import numpy as np
    import concourse.bacc as bacc
    from concourse.bass_utils import run_bass_kernel_spmd

    nc = bacc.Bacc("TRN2", target_bir_lowering=False, num_devices=1)
    arrays, args = {}, {}
    for name, a in lay_out({k: np.asarray(v) for k, v in inputs.items()}).items():
        arrays[f"in_{name}"] = np.ascontiguousarray(a)
        args[name] = nc.dram_tensor(f"in_{name}", a.shape, mybir.dt.from_np(a.dtype), kind="ExternalInput").ap()
    out = nc.dram_tensor("out", (T, P, D), F32, kind="ExternalOutput").ap()
    regions = nc.dram_tensor("regions", (E * R + SPARE * P, W), F32, kind="Internal").ap()
    picked = nc.dram_tensor("picked", (PICKED + 2 * SPARE * P, D), F32, kind="Internal").ap()
    tower_kernel(nc, out=out, regions=regions, picked=picked, **args)
    r = run_bass_kernel_spmd(nc, [arrays], core_ids=[0])
    return r.results[0]["out"]
```
